# Optimizing a Trainium2 kernel written in Bass

```python
import numpy as np
import jax
import jax.numpy as jnp

def _softmax(x, axis=-1):
    return jax.nn.softmax(x, axis=axis)

def _gelu(x):
    return jax.nn.gelu(x, approximate=True)

def _silu(x):
    return jax.nn.silu(x)

def _sigmoid(x):
    return jax.nn.sigmoid(x)

def _layernorm(x, axis=-1, eps=1e-05):
    m = jnp.mean(x, axis=axis, keepdims=True)
    v = jnp.var(x, axis=axis, keepdims=True)
    return (x - m) / jnp.sqrt(v + eps)

def _scatter_add(tgt, idx, src, axis=0):
    return tgt.at[idx].add(src)

def _segment_sum(src, seg, n):
    return jax.ops.segment_sum(src, seg, n)
kernel_name = 'mk_gnn_ffn_d2_gnn_r8_93c998'

def setup_inputs(seed: int=0):
    np.random.seed(seed)
    _w = jnp.asarray

    def _rec_inputs():
        import jax
        import jax.numpy as jnp
        _gk = jax.random.key(seed)
        x = -0.0003713 + 1 * jax.random.normal(jax.random.fold_in(_gk, 1), (6250, 256), jnp.float32)
        src = jax.random.randint(jax.random.fold_in(_gk, 2), (100000,), 0, 6250, jnp.int32)
        dst = jax.random.randint(jax.random.fold_in(_gk, 3), (100000,), 0, 6250, jnp.int32)
        _o = jnp.argsort(dst, stable=True)
        src = src[_o]
        dst = dst[_o]
        return (x, src, dst)
    x, src, dst = _rec_inputs()

    def _L0_gnn_setup():
        import jax, jax.numpy as jnp
        import numpy as np
        N = 6250
        DEG = 16
        E = N * DEG
        F = 256
        H = 8
        DH = 32
        ALPHA = 0.2
        key = jax.random.key(seed)
        ks = jax.random.split(key, 6)
        h = jax.random.normal(ks[0], (N, F), jnp.float32)
        lim_w = 1.414 * np.sqrt(6.0 / (F + DH))
        W = jax.random.uniform(ks[1], (H, F, DH), jnp.float32, -lim_w, lim_w)
        bW = jnp.zeros((H, DH), jnp.float32)
        lim_a = 1.414 * np.sqrt(6.0 / (2 * DH + 1))
        a_src = jax.random.uniform(ks[2], (H, DH), jnp.float32, -lim_a, lim_a)
        a_dst = jax.random.uniform(ks[3], (H, DH), jnp.float32, -lim_a, lim_a)
        a_bias = jnp.zeros((H,), jnp.float32)
        src = jax.random.randint(ks[4], (E,), 0, N, dtype=jnp.int32)
        dst = jnp.repeat(jnp.arange(N, dtype=jnp.int32), DEG)
        return {'h': h, 'W': W, 'bW': bW, 'a_src': a_src, 'a_dst': a_dst, 'a_bias': a_bias, 'src': src, 'dst': dst}
    _L0_gnn_all = _L0_gnn_setup()
    _L0_gnn_in = {k: v for k, v in _L0_gnn_all.items() if k in ('W', 'bW', 'a_src', 'a_dst', 'a_bias')}
    del _L0_gnn_all

    def _L0_ffn_setup():
        import jax, jax.numpy as jnp
        import numpy as np
        B, S, D, E, H, K = (4, 512, 256, 8, 512, 2)
        key = jax.random.key(seed)
        ks = jax.random.split(key, 6)
        x = jax.random.normal(ks[0], (B, S, D), jnp.float32)
        Wg = jax.random.normal(ks[1], (D, E), jnp.float32) * 0.02
        bg = jnp.zeros((E,), jnp.float32)
        W1 = jax.random.normal(ks[2], (E, D, H), jnp.float32) * 0.02
        b1 = jnp.zeros((E, H), jnp.float32)
        W2 = jax.random.normal(ks[3], (E, H, D), jnp.float32) * 0.02
        b2 = jnp.zeros((E, D), jnp.float32)
        return {'x': x, 'Wg': Wg, 'bg': bg, 'W1': W1, 'b1': b1, 'W2': W2, 'b2': b2}
    _L0_ffn_all = _L0_ffn_setup()
    _L0_ffn_in = {k: v for k, v in _L0_ffn_all.items() if k in ('Wg', 'bg', 'W1', 'b1', 'W2', 'b2')}
    del _L0_ffn_all

    def _L1_gnn_setup():
        import jax, jax.numpy as jnp
        import numpy as np
        N_NODES = 6250
        N_EDGES = 100000
        IN_F = 256
        HEADS = 8
        D = 32
        ALPHA_SLOPE = 0.2
        EPS = 1e-16
        key = jax.random.key(seed)
        k1, k2, k3, k4, k5 = jax.random.split(key, 5)
        x = jax.random.normal(k1, (N_NODES, IN_F), dtype=jnp.float32)
        W = jax.random.normal(k2, (HEADS, IN_F, D), dtype=jnp.float32) * 0.05
        a = jax.random.normal(k3, (HEADS, 5 * D), dtype=jnp.float32) * 0.05
        src = jax.random.randint(k4, (N_EDGES,), 0, N_NODES, dtype=jnp.int32)
        dst = jax.random.randint(k5, (N_EDGES,), 0, N_NODES, dtype=jnp.int32)
        return {'x': x, 'W': W, 'a': a, 'src': src, 'dst': dst}
    _L1_gnn_all = _L1_gnn_setup()
    _L1_gnn_in = {k: v for k, v in _L1_gnn_all.items() if k in ('W', 'a')}
    del _L1_gnn_all

    def _L1_ffn_setup():
        import jax, jax.numpy as jnp
        import numpy as np
        DIM = 256
        H = 8
        D = 64
        G = 64
        INNER = H * D
        SCALE = D ** (-0.5)
        key = jax.random.key(seed)
        ks = jax.random.split(key, 12)
        B, N = (4, 2048)
        x = jax.random.normal(ks[0], (B, N, DIM), dtype=jnp.float32)
        s = lambda fan_in: 1.0 / np.sqrt(fan_in)
        W_fx = jax.random.normal(ks[1], (DIM, INNER), dtype=jnp.float32) * s(DIM)
        b_fx = jnp.zeros((INNER,), dtype=jnp.float32)
        W_x = jax.random.normal(ks[2], (DIM, INNER), dtype=jnp.float32) * s(DIM)
        b_x = jnp.zeros((INNER,), dtype=jnp.float32)
        A = jax.random.normal(ks[3], (G, D), dtype=jnp.float32)
        Q, _ = jnp.linalg.qr(A.T)
        W_slice = Q[:, :G].astype(jnp.float32)
        b_slice = jnp.zeros((G,), dtype=jnp.float32)
        W_q = jax.random.normal(ks[4], (D, D), dtype=jnp.float32) * s(D)
        W_k = jax.random.normal(ks[5], (D, D), dtype=jnp.float32) * s(D)
        W_v = jax.random.normal(ks[6], (D, D), dtype=jnp.float32) * s(D)
        W_out = jax.random.normal(ks[7], (INNER, DIM), dtype=jnp.float32) * s(INNER)
        b_out = jnp.zeros((DIM,), dtype=jnp.float32)
        temperature = jnp.ones((1, H, 1, 1), dtype=jnp.float32) * 0.5
        return {'x': x, 'W_fx': W_fx, 'b_fx': b_fx, 'W_x': W_x, 'b_x': b_x, 'W_slice': W_slice, 'b_slice': b_slice, 'W_q': W_q, 'W_k': W_k, 'W_v': W_v, 'W_out': W_out, 'b_out': b_out, 'temperature': temperature}
    _L1_ffn_all = _L1_ffn_setup()
    _L1_ffn_in = {k: v for k, v in _L1_ffn_all.items() if k in ('W_fx', 'b_fx', 'W_x', 'b_x', 'W_slice', 'b_slice', 'W_q', 'W_k', 'W_v', 'W_out', 'b_out', 'temperature')}
    del _L1_ffn_all
    return {'x': x, 'src': src, 'dst': dst, 'L0_gnn_W': _L0_gnn_in['W'], 'L0_gnn_bW': _L0_gnn_in['bW'], 'L0_gnn_a_src': _L0_gnn_in['a_src'], 'L0_gnn_a_dst': _L0_gnn_in['a_dst'], 'L0_gnn_a_bias': _L0_gnn_in['a_bias'], 'L0_ffn_Wg': _L0_ffn_in['Wg'], 'L0_ffn_bg': _L0_ffn_in['bg'], 'L0_ffn_W1': _L0_ffn_in['W1'], 'L0_ffn_b1': _L0_ffn_in['b1'], 'L0_ffn_W2': _L0_ffn_in['W2'], 'L0_ffn_b2': _L0_ffn_in['b2'], 'L1_gnn_W': _L1_gnn_in['W'], 'L1_gnn_a': _L1_gnn_in['a'], 'L1_ffn_W_fx': _L1_ffn_in['W_fx'], 'L1_ffn_b_fx': _L1_ffn_in['b_fx'], 'L1_ffn_W_x': _L1_ffn_in['W_x'], 'L1_ffn_b_x': _L1_ffn_in['b_x'], 'L1_ffn_W_slice': _L1_ffn_in['W_slice'], 'L1_ffn_b_slice': _L1_ffn_in['b_slice'], 'L1_ffn_W_q': _L1_ffn_in['W_q'], 'L1_ffn_W_k': _L1_ffn_in['W_k'], 'L1_ffn_W_v': _L1_ffn_in['W_v'], 'L1_ffn_W_out': _L1_ffn_in['W_out'], 'L1_ffn_b_out': _L1_ffn_in['b_out'], 'L1_ffn_temperature': _L1_ffn_in['temperature']}

def reference(x, src, dst, L0_gnn_W, L0_gnn_bW, L0_gnn_a_src, L0_gnn_a_dst, L0_gnn_a_bias, L0_ffn_Wg, L0_ffn_bg, L0_ffn_W1, L0_ffn_b1, L0_ffn_W2, L0_ffn_b2, L1_gnn_W, L1_gnn_a, L1_ffn_W_fx, L1_ffn_b_fx, L1_ffn_W_x, L1_ffn_b_x, L1_ffn_W_slice, L1_ffn_b_slice, L1_ffn_W_q, L1_ffn_W_k, L1_ffn_W_v, L1_ffn_W_out, L1_ffn_b_out, L1_ffn_temperature):
    import jax
    import jax.numpy as jnp

    def _L0_gnn_ref(h, W, bW, a_src, a_dst, a_bias, src, dst):
        import jax, jax.numpy as jnp
        import numpy as np
        N = 6250
        DEG = 16
        E = N * DEG
        F = 256
        H = 8
        DH = 32
        ALPHA = 0.2
        Wh = jnp.einsum('nf,hfd->nhd', h, W) + bW
        s1 = jnp.einsum('nhd,hd->nh', Wh, a_src)
        s2 = jnp.einsum('nhd,hd->nh', Wh, a_dst)
        e = jax.nn.leaky_relu(s1[src] + s2[dst] + a_bias, ALPHA)
        m = jax.ops.segment_max(e, dst, num_segments=N)
        ex = jnp.exp(e - m[dst])
        denom = jax.ops.segment_sum(ex, dst, num_segments=N)
        attn = ex / denom[dst]
        hp = jax.ops.segment_sum(attn[:, :, None] * Wh[src], dst, num_segments=N)
        return hp.reshape(N, H * DH)

    def _L0_ffn_ref(x, Wg, bg, W1, b1, W2, b2):
        import jax, jax.numpy as jnp
        import numpy as np
        B, S, D, E, H, K = (4, 512, 256, 8, 512, 2)
        Bv, Sv, Dv = x.shape
        gate_scores = x @ Wg + bg
        _, idx = jax.lax.top_k(gate_scores, K)
        mask = jax.nn.one_hot(idx, E, dtype=x.dtype).sum(axis=-2)
        xf = x.reshape(-1, Dv)
        mf = mask.reshape(-1, E)
        h = jax.nn.gelu(jnp.einsum('td,edh->teh', xf, W1) + b1[None], approximate=False)
        y = jnp.einsum('teh,ehd->ted', h, W2) + b2[None]
        out = jnp.einsum('ted,te->td', y, mf)
        return out.reshape(Bv, Sv, Dv)

    def _L1_gnn_ref(x, W, a, src, dst):
        import jax, jax.numpy as jnp
        import numpy as np
        N_NODES = 6250
        N_EDGES = 100000
        IN_F = 256
        HEADS = 8
        D = 32
        ALPHA_SLOPE = 0.2
        EPS = 1e-16
        n = x.shape[0]
        h = jnp.einsum('ni,hio->nho', x, W)
        hs = h[src]
        hd = h[dst]
        diff = hd - hs
        a1, a2, a3, a4, a5 = jnp.split(a, 5, axis=1)
        lin = jnp.einsum('ehd,hd->eh', hs, a1) + jnp.einsum('ehd,hd->eh', hd, a2) + jnp.einsum('ehd,hd->eh', diff, a3) + jnp.einsum('ehd,hd->eh', jnp.abs(diff), a4) + jnp.einsum('ehd,hd->eh', hs * hd, a5)
        alpha = jnp.where(lin > 0, lin, ALPHA_SLOPE * lin)
        mx = jax.ops.segment_max(alpha, src, num_segments=n)
        e = jnp.exp(alpha - mx[src])
        s = jax.ops.segment_sum(e, src, num_segments=n)
        att = e / (s[src] + EPS)
        out = jax.ops.segment_sum(att[..., None] * hd, src, num_segments=n)
        return out.reshape(n, HEADS * D)

    def _L1_ffn_ref(x, W_fx, b_fx, W_x, b_x, W_slice, b_slice, W_q, W_k, W_v, W_out, b_out, temperature):
        import jax, jax.numpy as jnp
        import numpy as np
        DIM = 256
        H = 8
        D = 64
        G = 64
        INNER = H * D
        SCALE = D ** (-0.5)
        B, N, _ = x.shape
        fx_mid = (x @ W_fx + b_fx).reshape(B, N, H, D).transpose(0, 2, 1, 3)
        x_mid = (x @ W_x + b_x).reshape(B, N, H, D).transpose(0, 2, 1, 3)
        temp = jnp.clip(temperature, 0.1, 5.0)
        slice_weights = jax.nn.softmax((x_mid @ W_slice + b_slice) / temp, axis=-1)
        slice_norm = slice_weights.sum(axis=2)
        slice_token = jnp.einsum('bhnc,bhng->bhgc', fx_mid, slice_weights)
        slice_token = slice_token / (slice_norm[..., None] + 1e-05)
        q = slice_token @ W_q
        k = slice_token @ W_k
        v = slice_token @ W_v
        attn = jax.nn.softmax(jnp.einsum('bhgc,bhkc->bhgk', q, k) * SCALE, axis=-1)
        out_slice = jnp.einsum('bhgk,bhkc->bhgc', attn, v)
        out_x = jnp.einsum('bhgc,bhng->bhnc', out_slice, slice_weights)
        out_x = out_x.transpose(0, 2, 1, 3).reshape(B, N, INNER)
        return out_x @ W_out + b_out
    x = x + _L0_gnn_ref(_layernorm(x, axis=-1), L0_gnn_W, L0_gnn_bW, L0_gnn_a_src, L0_gnn_a_dst, L0_gnn_a_bias, src, dst)
    x = x + _L0_ffn_ref(_layernorm(x, axis=-1)[None], L0_ffn_Wg, L0_ffn_bg, L0_ffn_W1, L0_ffn_b1, L0_ffn_W2, L0_ffn_b2)[0]
    x = x + _L1_gnn_ref(_layernorm(x, axis=-1), L1_gnn_W, L1_gnn_a, src, dst)
    x = x + _L1_ffn_ref(_layernorm(x, axis=-1)[None], L1_ffn_W_fx, L1_ffn_b_fx, L1_ffn_W_x, L1_ffn_b_x, L1_ffn_W_slice, L1_ffn_b_slice, L1_ffn_W_q, L1_ffn_W_k, L1_ffn_W_v, L1_ffn_W_out, L1_ffn_b_out, L1_ffn_temperature)[0]
    return x

_drawn_inputs = setup_inputs


def setup_inputs(seed=0):
    import zlib

    import numpy as np

    out = dict(_drawn_inputs(seed))
    spreads = {'L0_gnn_bW': (0.0, 0.1),
     'L0_gnn_a_bias': (0.0, 0.553),
     'L0_ffn_bg': (0.0, 0.1),
     'L0_ffn_b1': (0.0, 0.344),
     'L0_ffn_b2': (0.0, 0.1),
     'L1_ffn_b_fx': (0.0, 0.1),
     'L1_ffn_b_x': (0.0, 0.8),
     'L1_ffn_b_slice': (0.0, 0.8),
     'L1_ffn_b_out': (0.0, 0.1),
     'L1_ffn_temperature': (0.5, 0.6)}
    factors = {'L1_ffn_W_x': 8.0, 'L1_ffn_W_slice': 8.0, 'L1_ffn_W_q': 8.0, 'L1_ffn_W_k': 8.0}
    for name, (base, spread) in spreads.items():
        noise = np.random.default_rng([zlib.crc32(name.encode()), seed]).standard_normal(out[name].shape)
        drawn = base * np.exp(spread * noise) if base else spread * noise
        out[name] = jnp.asarray(drawn.astype(out[name].dtype))
    for name, factor in factors.items():
        out[name] = (out[name] * factor).astype(out[name].dtype)
    return out
```

```python
from contextlib import ExitStack

import concourse.bass as bass
from concourse import mybir

ALU = mybir.AluOpType
ACT = mybir.ActivationFunctionType
AX = mybir.AxisListType
F32 = mybir.dt.float32
BF16 = mybir.dt.bfloat16
I32 = mybir.dt.int32
U32 = mybir.dt.uint32

P = 128
N, F = 6250, 256
H, DH = 8, 32
E = 100000
FC = F // P
NT = -(-N // P)
TAIL = N - (NT - 1) * P
LANES, COLS = 125, 800
assert LANES * COLS == E
RING = 8
ET = -(-((E + NT * (P - 1)) // P) // RING) * RING
GW = F + H
VW = DH + 1
EPS_LN = 1e-5
EPS_S = 1e-16
SLOPE = 0.2
CODE = 8
KC = H + CODE + 1
MB = 15
BIG = float(2 ** 20)
XP = 8
HID = 512
HC = HID // P
SG, SD = 64, 64
INNER = H * SD


class Pack:

    whole = None
    layer = None

    def __init__(self, nc, stack):
        self.nc, self.stack = nc, stack

    def sb(self, name, shape, dt=F32):
        return self.stack.enter_context(self.nc.sbuf_tensor(name, shape, dt))

    def ps(self, name, shape, dt=F32):
        return self.stack.enter_context(self.nc.psum_tensor(name, shape, dt))

    def sem(self, name):
        s = Pack.layer[1].enter_context(self.nc.semaphore(name))
        Pack.layer[0].append(s)
        return s

    def pool_dma_sem(self, name):
        return Pack.whole.enter_context(self.nc.semaphore(name))


class Link:

    def __init__(self, eng, sem):
        self.eng, self.sem, self.n = eng, sem, 0

    def __call__(self, ins):
        self.n += 1
        ins.then_inc(self.sem, 1)
        self.eng.wait_ge(self.sem, self.n)


def end_layer(nc):
    sems, stack = Pack.layer
    with nc.Block() as block:
        @block.gpsimd
        def _(pool):
            for s in sems:
                pool.sem_clear(s)
    stack.close()
    Pack.layer = ([], stack)


def constants(nc, top):
    c = {}
    c["ident"] = top.sb("ident", [P, P])
    c["sel"] = top.sb("sel", [KC, H, P], BF16)
    c["slot"] = top.sb("slot_row", [P, P])
    c["bits"] = top.sb("bits", [P, 1, CODE], I32)
    c["iota"] = top.sb("iota_row", [P, P])
    c["ones"] = top.sb("ones", [P, P])
    c["zeros"] = top.sb("zeros", [P, P])
    s = top.sem("consts_made")
    with nc.Block() as block:
        @block.gpsimd
        def _(pool):
            pool.memset(c["ident"][:, :], 0.0).then_inc(s, 1)
            pool.memset(c["ones"][:, :], 1.0)
            pool.memset(c["zeros"][:, :], 0.0)
            pool.iota(c["iota"][:, :], pattern=[[1, P]], base=0, channel_multiplier=0,
                      allow_small_or_imprecise_dtypes=True)
            pool.wait_ge(s, 1)
            pool.affine_select(out=c["ident"][:, :], in_=c["ident"][:, :], compare_op=ALU.not_equal,
                               fill=1.0, base=0, pattern=[[-1, P]], channel_multiplier=1)
            pool.iota(c["slot"][:, :], pattern=[[1, P]], base=2 * P, channel_multiplier=0,
                      allow_small_or_imprecise_dtypes=True)
    selectors(nc, c)
    return c


def triangles(nc, m, c):
    c["before"] = m.sb("before", [P, P])
    c["upto"] = m.sb("upto", [P, P])
    cleared = m.sem("triangles_cleared")
    with nc.Block() as block:
        @block.gpsimd
        def _(pool):
            pool.memset(c["before"][:, :], 0.0).then_inc(cleared, 1)
            pool.memset(c["upto"][:, :], 0.0).then_inc(cleared, 1)
            pool.wait_ge(cleared, 2)
            for name, cmp in (("before", ALU.is_ge), ("upto", ALU.is_gt)):
                pool.affine_select(out=c[name][:, :], in_=c[name][:, :], compare_op=cmp, fill=1.0,
                                   base=0, pattern=[[-1, P]], channel_multiplier=1)


def selectors(nc, c):
    with ExitStack() as st:
        m = Pack(nc, st)
        node = m.sb("node_no", [P, CODE], I32)
        bits = m.sb("low_bits", [P, CODE], I32)
        on = m.sb("bits_on", [P, CODE])
        weight = m.sb("bit_weights", [P, CODE])
        col = m.sb("sel_columns", [P, H, KC])
        banks = [m.ps(f"p_sel{i}", [P, 512]) for i in range(2)]
        numbered, link_sem, made, turned = (m.sem(n) for n in ("nodes_numbered", "sel_link", "sel_made",
                                                               "sel_turned"))
        with nc.Block() as block:
            @block.gpsimd
            def _(pool):
                pool.iota(node[:, :], pattern=[[0, CODE]], base=0, channel_multiplier=1)\
                    .then_inc(numbered, 1)

            @block.vector
            def _(dve):
                link = Link(dve, link_sem)
                link(dve.memset(col[:, :, :], 0.0))
                for b in range(CODE):
                    dve.memset(bits[:, b:b + 1], 1 << b)
                    dve.memset(c["bits"][:, :, b:b + 1], 1 << (MB + b))
                    dve.memset(weight[:, b:b + 1], BIG / 2 ** (MB + b))
                for h in range(H):
                    link(dve.memset(col[:, h, h:h + 1], 1.0))
                dve.wait_ge(numbered, 1)
                link(dve.tensor_tensor(node[:, :], node[:, :], bits[:, :], ALU.bitwise_and))
                link(dve.tensor_copy(on[:, :], node[:, :]))
                link(dve.tensor_single_scalar(on[:, :], on[:, :], 1.0, ALU.min))
                link(dve.tensor_reduce(col[:, 0, KC - 1:KC], on[:, :], AX.X, ALU.add))
                link(dve.tensor_single_scalar(col[:, 0, KC - 1:KC], col[:, 0, KC - 1:KC], -BIG, ALU.mult))
                link(dve.tensor_scalar(on[:, :], on[:, :], 2.0, -1.0, ALU.mult, ALU.add))
                link(dve.tensor_tensor(col[:, 0, H:KC - 1], on[:, :], weight[:, :], ALU.mult))
                for h in range(1, H):
                    link(dve.tensor_copy(col[:, h, H:KC], col[:, 0, H:KC]))
                dve.sem_inc(made, 1)
                dve.wait_ge(turned, 1)
                for i in range(2):
                    link(dve.tensor_copy(c["sel"][:, i * 4:(i + 1) * 4, :].rearrange("k h n -> k (h n)"),
                                         banks[i][0:KC, :]))

            @block.tensor
            def _(pe):
                pe.wait_ge(made, 1)
                for h in range(H):
                    mm = pe.transpose(banks[h // 4][0:KC, h % 4 * P:(h % 4 + 1) * P], col[:, h, :],
                                      c["ident"][:, :])
                mm.then_inc(turned, 1)



class Order:

    def __init__(self, nc, top, tag, key, other):
        self.tag, self.key, self.other = tag, key, other
        self.pay = top.sb(f"pay{tag}", [LANES, COLS, 2], I32)
        self.addr = top.sb(f"addr{tag}", [LANES, COLS], I32)
        self.sorted = nc.dram_tensor(f"sorted{tag}", (P * ET, 2), I32).ap()
        self.loaded = top.sem(f"edges_loaded{tag}")
        self.padded = top.sem(f"list_padded{tag}")
        self.link = top.sem(f"order_link{tag}")
        self.counted = top.sem(f"counted{tag}")
        self.summed = top.sem(f"summed{tag}")
        self.tiles = top.sem(f"tiles{tag}")
        self.ends = top.sem(f"ends{tag}")
        self.ge = top.sem(f"ge{tag}")
        self.ids = top.sem(f"ids{tag}")
        self.scattered = [top.pool_dma_sem(f"scattered{tag}{h}") for h in range(2)]
        self.staged = top.sem(f"staged{tag}")
        self.passed = top.sem(f"passed{tag}")


def order_buffers(top, tag, o):
    b = {}
    o.key_i = top.sb(f"key{tag}", [LANES, COLS], I32)
    o.other_i = top.sb(f"other{tag}", [LANES, COLS], I32)
    b["hi"] = top.sb(f"hi{tag}", [LANES, COLS])
    b["tmp"] = top.sb(f"tmp{tag}", [LANES, COLS], I32)
    b["hit"] = top.sb(f"hit{tag}", [LANES, COLS], I32)
    b["run"] = top.sb(f"run{tag}", [LANES, COLS])
    b["pos"] = top.sb(f"pos{tag}", [LANES, COLS])
    b["zero"] = top.sb(f"zerorow{tag}", [LANES, COLS])
    b["cnt"] = top.sb(f"cnt{tag}", [LANES, NT])
    b["tile_i"] = top.sb(f"tile_i{tag}", [P, NT], I32)
    b["tile_f"] = top.sb(f"tile_f{tag}", [P, NT])
    b["end_f"] = top.sb(f"end_f{tag}", [P, NT])
    b["base"] = top.sb(f"base{tag}", [P, NT])
    b["coli"] = top.sb(f"coli{tag}", [NT, 1], I32)
    b["colf"] = top.sb(f"colf{tag}", [NT, 1])
    b["endc"] = top.sb(f"endc{tag}", [NT, 1])
    b["tcount"] = top.sb(f"tcount{tag}", [NT, ET])
    b["ge"] = top.sb(f"gerow{tag}", [NT, ET])
    b["p_tid0"] = top.ps(f"p_tid0{tag}", [P, 512])
    b["p_tid1"] = top.ps(f"p_tid1{tag}", [P, 512])
    small = top.ps(f"p_small{tag}", [P, 512])
    b["p_tot"], b["p_pre"], b["p_col"] = small[:, 0:64], small[:, 64:128], small[:, 128:130]
    return b


def order_loads(eng, o, padrow):
    eng.dma_start(o.key_i[:, :], o.key.rearrange("(p j) -> p j", p=LANES)).then_inc(o.loaded, 16)
    eng.dma_start(o.other_i[:, :], o.other.rearrange("(p j) -> p j", p=LANES)).then_inc(o.loaded, 16)
    eng.dma_start(o.sorted.rearrange("(p t) c -> p t c", p=P), padrow).then_inc(o.padded, 16)


def order_vector(dve, o, b, c, tid_row):
    link = Link(dve, o.link)
    dve.wait_ge(o.loaded, 32)
    link(dve.tensor_single_scalar(b["tmp"][:, :], o.key_i[:, :], 7, ALU.arith_shift_right))
    link(dve.tensor_copy(b["hi"][:, :], b["tmp"][:, :]))
    link(dve.tensor_single_scalar(b["tmp"][:, :], o.key_i[:, :], P - 1, ALU.bitwise_and))
    link(dve.tensor_scalar(o.pay[:, :, 0].bitcast(F32), b["tmp"][:, :], float(2 * P), None, ALU.add))
    link(dve.tensor_copy(o.pay[:, :, 1], o.other_i[:, :]))
    link(dve.memset(b["zero"][:, :], 0.0))
    link(dve.memset(b["pos"][:, :], 0.0))
    n = link.n
    with dve.Fori(0, NT) as k:
        dve.wait_ge(o.link, k + n)
        dve.tensor_scalar(b["hit"][:, :], b["hi"][:, :], c["iota"][0:LANES, bass.ds(k, 1)], 0.0,
                          ALU.is_equal, ALU.add, accum_out=b["cnt"][:, bass.ds(k, 1)]).then_inc(o.link, 1)
    link.n += NT
    dve.wait_ge(o.link, link.n)
    dve.sem_inc(o.counted, 1)
    dve.wait_ge(o.summed, 1)
    link(dve.tensor_scalar(b["tile_i"][:, :], b["p_tot"][:, 0:NT], float(P - 1), None, ALU.add))
    link(dve.tensor_single_scalar(b["tile_i"][:, :], b["tile_i"][:, :], 7, ALU.arith_shift_right))
    link(dve.tensor_copy(b["tile_f"][:, :], b["tile_i"][:, :]))
    link(dve.tensor_scalar(b["coli"][:, :], b["p_col"][0:NT, 0:1], float(P - 1), None, ALU.add))
    link(dve.tensor_single_scalar(b["coli"][:, :], b["coli"][:, :], 7, ALU.arith_shift_right))
    link(dve.tensor_copy(b["colf"][:, :], b["coli"][:, :]))
    dve.sem_inc(o.tiles, 1)
    link(dve.tensor_tensor_scan(b["end_f"][:, :], b["tile_f"][:, :], c["zeros"][:, 0:NT], 0.0,
                                ALU.add, ALU.add))
    link(dve.tensor_tensor(b["base"][:, :], b["end_f"][:, :], b["tile_f"][:, :], ALU.subtract))
    link(dve.tensor_scalar(b["base"][:, :], b["base"][:, :], float(P), -1.0, ALU.mult, ALU.add))
    dve.wait_ge(o.ends, 1)
    link(dve.tensor_tensor(b["base"][0:LANES, :], b["base"][0:LANES, :], b["p_pre"][0:LANES, 0:NT],
                           ALU.add))
    link(dve.tensor_copy(b["endc"][:, :], b["p_col"][0:NT, 1:2]))
    link(dve.tensor_scalar(b["ge"][:, :], b["tcount"][:, :], b["endc"][:, 0:1], None, ALU.is_ge))
    dve.sem_inc(o.ge, 1)
    half = ET // 2
    for h, bank in enumerate(("p_tid0", "p_tid1")):
        dve.wait_ge(o.ids, 1)
        link(dve.tensor_copy(tid_row[0:1, h * half:(h + 1) * half], b[bank][0:1, 0:half]))
    n = link.n
    with dve.Fori(0, NT) as k:
        dve.wait_ge(o.link, k * 3 + n)
        dve.tensor_scalar(b["hit"][:, :], b["hi"][:, :], c["iota"][0:LANES, bass.ds(k, 1)], None,
                          ALU.is_equal).then_inc(o.link, 1)
        dve.wait_ge(o.link, k * 3 + (n + 1))
        dve.tensor_tensor_scan(b["run"][:, :], b["hit"][:, :], b["zero"][:, :],
                               b["base"][0:LANES, bass.ds(k, 1)], ALU.add, ALU.add).then_inc(o.link, 1)
        dve.wait_ge(o.link, k * 3 + (n + 2))
        dve.sem_inc(o.passed, 1)
        dve.copy_predicated(b["pos"][:, :], b["hit"][:, :], b["run"][:, :]).then_inc(o.link, 1)
    link.n += 3 * NT
    dve.wait_ge(o.link, link.n)
    link(dve.tensor_copy(b["tmp"][:, :], b["pos"][:, :]))
    link(dve.tensor_single_scalar(b["hit"][:, :], b["tmp"][:, :], P - 1, ALU.bitwise_and))
    link(dve.tensor_copy(b["hi"][:, :], b["hit"][:, :]))
    link(dve.tensor_single_scalar(b["hit"][:, :], b["tmp"][:, :], 7, ALU.arith_shift_right))
    link(dve.tensor_copy(b["run"][:, :], b["hit"][:, :]))
    link(dve.scalar_tensor_tensor(out=o.addr[:, :], in0=b["hi"][:, :], scalar=float(ET),
                                  in1=b["run"][:, :], op0=ALU.mult, op1=ALU.add))


def order_tensor(pe, o, b, c):
    pe.wait_ge(o.counted, 1)
    pe.matmul(b["p_tot"][:, 0:NT], c["ones"][0:LANES, :], b["cnt"][:, :], start=True, stop=True)
    pe.matmul(b["p_pre"][0:LANES, 0:NT], c["before"][0:LANES, 0:LANES], b["cnt"][:, :],
              start=True, stop=True)
    pe.matmul(b["p_col"][0:NT, 0:1], b["cnt"][:, :], c["ones"][0:LANES, 0:1],
              start=True, stop=True).then_inc(o.summed, 1)
    pe.wait_ge(o.tiles, 1)
    pe.matmul(b["p_col"][0:NT, 1:2], c["upto"][0:NT, 0:NT], b["colf"][:, :],
              start=True, stop=True).then_inc(o.ends, 1)
    pe.wait_ge(o.ge, 1)
    half = ET // 2
    for h, bank in enumerate(("p_tid0", "p_tid1")):
        mm = pe.matmul(b[bank][0:1, 0:half], c["ones"][0:NT - 1, 0:1],
                       b["ge"][0:NT - 1, h * half:(h + 1) * half], start=True, stop=True)
    mm.then_inc(o.ids, 1)


def order_scatter(pool, o, stage):
    W = RING
    idx, pay = stage
    pool.wait_ge(o.padded, 16)

    def half(it, h):
        pool.tensor_copy(idx[:, h, :], o.addr[:, bass.ds(it * (2 * W) + h * W, W)])\
            .then_inc(o.staged, 1)
        pool.tensor_copy(pay[:, h, :, :], o.pay[:, bass.ds(it * (2 * W) + h * W, W), :])\
            .then_inc(o.staged, 1)
        pool.wait_ge(o.staged, it * 4 + (2 * h + 2))
        pool.sem_inc(o.passed, 1)
        for k in range(W):
            pool.indirect_dma_start(o.sorted, bass.IndirectOffsetOnAxis(ap=idx[:, h, k:k + 1], axis=0),
                                    pay[:, h, k, :], None).then_inc(o.scattered[h], 16)

    steps = COLS // (2 * W)
    half(0, 0)
    half(0, 1)
    with pool.Fori(1, steps) as it:
        for h in range(2):
            pool.wait_ge(o.scattered[h], it * (16 * W))
            pool.sem_inc(o.passed, 1)
            half(it, h)
    for h in range(2):
        pool.wait_ge(o.scattered[h], steps * 16 * W)


def sort_buffers(nc, stack, tag, o):
    m = Pack(nc, stack)
    b = order_buffers(m, tag, o)
    pads = m.sb(f"pads{tag}", [P, ET, 2], I32)
    made = m.sem(f"pads_made{tag}")
    with nc.Block() as block:
        @block.vector
        def _(dve):
            dve.memset(pads[:, :, 0].bitcast(F32), float(2 * P + P)).then_inc(made, 1)
            dve.memset(pads[:, :, 1], N).then_inc(made, 1)

        @block.gpsimd
        def _(pool):
            pool.iota(b["tcount"][:, :], pattern=[[1, ET]], base=0, channel_multiplier=0,
                      allow_small_or_imprecise_dtypes=True)

        @block.sync
        def _(sp):
            sp.wait_ge(made, 2)
            order_loads(sp, o, pads[:, :, :])
            sp.wait_ge(o.loaded, 32)
            sp.wait_ge(o.padded, 16)
    return b


def sort_positions(nc, tag, c, o, tid_row):
    with ExitStack() as st:
        b = sort_buffers(nc, st, tag, o)
        with nc.Block() as block:
            @block.vector
            def _(dve):
                order_vector(dve, o, b, c, tid_row)

            @block.tensor
            def _(pe):
                order_tensor(pe, o, b, c)



def norm_stats(nc, top, tag, x, mv, rstd, save=None):
    with ExitStack() as st:
        m = Pack(nc, st)
        stats = m.sb(f"stats{tag}", [P, NT, 6])
        root = m.sb(f"root{tag}", [P, NT])
        eps = m.sb(f"eps{tag}", [P, 1])
        saved = m.sem(f"x_saved{tag}")
        did, var_ready, rooted = (m.sem(f"norm_{n}{tag}") for n in ("stat_done", "var_ready", "rooted"))
        with nc.Block() as block:
            @block.vector
            def _(dve):
                dve.memset(eps[:, :], EPS_LN).then_inc(var_ready, 1)
                with dve.Fori(0, NT) as t:
                    dve.bn_stats(stats[:, bass.ds(t, 1), :].rearrange("p a b -> p (a b)"),
                                 x[:, bass.ds(t, 1), :].rearrange("p a b -> p (a b)")).then_inc(did, 1)
                dve.wait_ge(did, NT)
                for t in range(NT):
                    a = dve.bn_aggr(mv[:, t, :], stats[:, t, :])
                a.then_inc(var_ready, 1)
                dve.wait_ge(rooted, 1)
                dve.reciprocal(rstd[:, :], root[:, :])

            @block.scalar
            def _(act):
                act.wait_ge(var_ready, 2)
                act.activation(root[:, :], mv[:, :, 1], ACT.Sqrt, bias=eps[:, 0:1]).then_inc(rooted, 1)

            @block.sync
            def _(sp):
                if save is not None:
                    sp.dma_start(node_dram(save), x[:, :, :]).then_inc(saved, 16)
                    sp.wait_ge(saved, 16)


def pairs(eng, count, body):
    with eng.Fori(0, count // 2) as it:
        body(it * 2, 0)
        body(it * 2 + 1, 1)
    if count % 2:
        body(count - 1, 0)


def tile_of(a, t):
    if isinstance(t, int):
        return a[:, t, :]
    return a[:, bass.ds(t, 1), :].rearrange("p a b -> p (a b)")


def col_of(a, t):
    return a[:, t:t + 1] if isinstance(t, int) else a[:, bass.ds(t, 1)]


def project(nc, tag, c, x, mv, rstd, wcat, brow, width, evacuate, extra=None):
    with ExitStack() as st:
        m = Pack(nc, st)
        xn = m.sb(f"xn{tag}", [P, 2, F])
        xt = m.sb(f"xt{tag}", [P, 2, FC, P])
        tps = [m.ps(f"tps{tag}{i}", [P, 512])[:, 0:F].rearrange("p (f n) -> p f n", f=FC)
               for i in range(2)]
        prj = [m.ps(f"prj{tag}{i}", [P, 512]) for i in range(2)]
        names = ("xn_ready", "xn_free", "turned", "xt_ready", "out_ready", "rows_ready",
                 "hold")
        s = {n: m.sem(f"proj_{n}{tag}") for n in names}
        with nc.Block() as block:
            @block.vector
            def _(dve):
                def body(t, k):
                    dve.wait_ge(s["xn_free"], t + 1)
                    dve.tensor_scalar(xn[:, k, :], tile_of(x, t), col_of(mv[:, :, 0], t),
                                      col_of(rstd, t), ALU.subtract, ALU.mult).then_inc(s["xn_ready"], 1)
                pairs(dve, NT, body)
                if extra:
                    extra["vector"](dve, s["rows_ready"])

            @block.scalar
            def _(act):
                def turned(t, k):
                    act.wait_ge(s["turned"], t + 1)
                    act.activation(xt[:, k, :, :], tps[k], ACT.Copy).then_inc(s["xt_ready"], 1)

                def emptied(t, k):
                    act.wait_ge(s["out_ready"], t + 1)
                    act.sem_inc(s["hold"], 1)
                    evacuate(act, t, k, prj[k]).then_inc(s["rows_ready"], 1)

                def body(t, k):
                    turned(t + 1, 1 - k)
                    emptied(t, k)
                turned(0, 0)
                pairs(act, NT - 1, body)
                emptied(NT - 1, (NT - 1) % 2)

            @block.tensor
            def _(pe):
                pe.sem_inc(s["xn_free"], 2)

                def turn(t, k):
                    pe.wait_ge(s["xn_ready"], t + 1)
                    if not isinstance(t, int) or t >= 2:
                        pe.wait_ge(s["xt_ready"], t - 1)
                    for f in range(FC):
                        mm = pe.transpose(tps[k][:, f, :], xn[:, k, f * P:(f + 1) * P], c["ident"][:, :])
                    mm.then_inc(s["turned"], 1)

                def multiply(t, k):
                    pe.wait_ge(s["xt_ready"], t + 1)
                    pe.sem_inc(s["xn_free"], 1)
                    if not isinstance(t, int) or t >= 2:
                        pe.wait_ge(s["rows_ready"], t - 1)
                    if brow is not None:
                        pe.matmul(prj[k][:, 0:width], c["ones"][0:1, :], brow[0:1, 0:width],
                                  start=True, stop=False)
                    for f in range(FC):
                        mm = pe.matmul(prj[k][:, 0:width], xt[:, k, f, :], wcat[:, f, 0:width],
                                       start=(brow is None and f == 0), stop=(f == FC - 1))
                    mm.then_inc(s["out_ready"], 1)

                def body(t, k):
                    turn(t + 1, 1 - k)
                    multiply(t, k)
                turn(0, 0)
                turn(1, 1)
                multiply(0, 0)
                turn(2, 0)
                multiply(1, 1)
                with pe.Fori(1, (NT - 1) // 2) as it:
                    body(it * 2, 0)
                    body(it * 2 + 1, 1)
                multiply(NT - 1, (NT - 1) % 2)
                if extra:
                    extra["tensor"](pe)

            @block.gpsimd
            def _(pool):
                if extra:
                    extra["gpsimd"](pool, s["rows_ready"])


def edge_phase(nc, tag, c, order, tid_row, table, acc, key8, key_parts=None, a45=None):
    pairwise = key_parts is not None
    R = RING
    width = GW + F if pairwise else GW
    DRAIN = RING
    with ExitStack() as st:
        m = Pack(nc, st)
        lst = m.sb(f"list{tag}", [P, ET, 2], I32)
        idx = m.sb(f"idx{tag}", [P, 2, R // 2], I32)
        got = m.sb(f"got{tag}", [P, R, width])
        hot = m.sb(f"hot{tag}", [P, R, P])
        hot_t = m.sb(f"hot_t{tag}", [P, R, P], BF16)
        lg = m.sb(f"lg{tag}", [P, R, KC])
        bits = m.sb(f"code{tag}", [P, R, CODE], I32)
        whole = m.sb(f"whole{tag}", [P, 2, H])
        below = m.sb(f"below{tag}", [P, 2, H])
        lg_t = m.sb(f"lg_t{tag}", [KC, 2, P], BF16)
        apart = m.sb(f"apart{tag}", [P, 2, P])
        tmax = m.sb(f"tmax{tag}", [P, 2, H])
        drop = m.sb(f"drop{tag}", [P, 2, 2, H])
        scale = m.sb(f"scale{tag}", [P, 4, H])
        wv = m.sb(f"wv{tag}", [P, 4, H, VW])
        mrun = m.sb(f"mrun{tag}", [P, NT, H], BF16)
        if pairwise:
            pair = m.sb(f"pair{tag}", [P, 2, 2, F])
            dot = m.sb(f"dot{tag}", [P, 4, H])
        p_turn, p_x, p_lgt, p_z, p_sum0, p_more = (
            m.ps(f"{n}{tag}", [P, 512]) for n in ("p_turn", "p_x", "p_lgt", "p_z", "p_sum", "p_more"))
        p_pair, p_sum = (p_more, [p_sum0]) if pairwise else (None, [p_sum0, p_more])
        p_max = m.ps(f"p_max{tag}", [P, H, P])
        names = ("list_in", "cleared", "staged", "bits_in", "coded", "passed",
                 "selected", "turned", "copied", "rowed",
                 "differed", "absed", "mixing", "mixed", "dotted", "termed", "joined",
                 "leaked", "lgt", "lgt_in", "spread",
                 "tmax_in", "rise_in", "mrun_in", "ramped", "scaled", "offset",
                 "below_in", "apart_in", "held", "ex_in",
                 "weighted", "sums", "faded", "added")
        s = {n: m.sem(f"edge_{n}{tag}") for n in names}
        arrived = [m.pool_dma_sem(f"arrived{tag}{i}") for i in range(R)]
        lo = lst[:, :, 0].bitcast(F32)

        class At:

            def __init__(self, it, k, lag, ids=None):
                j = k - lag
                self.slot = j % R
                self.t = it * R + j
                self.first = isinstance(it, int) and self.t == 0
                self.live = not isinstance(it, int) or 0 <= self.t < ET
                self.round = it + j // R
                if ids is not None and self.live:
                    self.tid = ids[j]
                self.n = self.t + 1

        def node_tiles(eng, engine, it):
            lo_, hi_ = (0 if isinstance(it, int) and it == 0 else -DRAIN,
                        0 if isinstance(it, int) and it > 0 else R)
            first = it * R + lo_
            row = tid_row[0:1, first:first + hi_ - lo_] if isinstance(it, int) \
                else tid_row[0:1, bass.ds(first, hi_ - lo_)]
            _, values = nc.values_load_multi_w_load_instructions(
                row, engines=[engine], min_val=0, max_val=NT - 1,
                skip_runtime_bounds_check_because="a sum of NT - 1 comparisons, each 0 or 1")
            return {lo_ + i: v for i, v in enumerate(values)}

        def steps(eng, body, engine=None):
            def one(it, n):
                ids = node_tiles(eng, engine, it) if engine is not None else None
                for k in range(n):
                    body(it, k, ids)
            one(0, R)
            with eng.Fori(1, ET // R) as it:
                one(it, R)
            one(ET // R, DRAIN)

        def run_stages(stages):
            def body(it, k, ids):
                for lag, stage in stages:
                    a = At(it, k, lag, ids)
                    if a.live and stage is not None:
                        stage(a)
            return body

        def node(table, a):
            return table[:, bass.ds(a.tid, 1), :].rearrange("p a b -> p (a b)")

        with nc.Block() as block:
            @block.sync
            def _(sp):
                sp.dma_start(lst[:, :, :], order.sorted.rearrange("(p t) c -> p t c", p=P))\
                    .then_inc(s["list_in"], 16)

            @block.gpsimd
            def _(pool):
                pool.wait_ge(s["list_in"], 16)
                W = R // 2

                def stage(it, h):
                    start = it * R + h * W
                    cols = slice(start, start + W) if isinstance(it, int) else bass.ds(start, W)
                    pool.tensor_copy(idx[:, h, :], lst[:, cols, 1]).then_inc(s["staged"], 1)
                    pool.wait_ge(s["staged"], it * 2 + (h + 1))
                    pool.sem_inc(s["passed"], 1)

                def encode(it, h):
                    half = slice(h * W, (h + 1) * W)
                    pool.wait_ge(s["bits_in"], it * 2 + (h + 1))
                    pool.sem_inc(s["passed"], 1)
                    pool.tensor_copy(lg[:, half, H:KC - 1], bits[:, half, :]).then_inc(s["coded"], 1)

                def gather(k):
                    pool.indirect_dma_start(
                        got[:, k, :], None, table,
                        bass.IndirectOffsetOnAxis(ap=idx[:, k // W, k % W:k % W + 1], axis=0),
                    ).then_inc(arrived[k], 16)

                def weigh(a):
                    q = a.slot % 4
                    pool.wait_ge(s["ex_in"], a.n)
                    pool.tensor_tensor(wv[:, q, :, 0:DH],
                                       got[:, a.slot, 0:F].rearrange("p (h d) -> p h d", h=H),
                                       wv[:, q, :, DH:VW].to_broadcast([P, H, DH]), ALU.mult)\
                        .then_inc(s["weighted"], 1)

                def mix(a):
                    k = a.slot % 2
                    pool.wait_ge(s["absed"], a.n)
                    pool.tensor_tensor(pair[:, k, 0, :], pair[:, k, 0, :], a45[:, 0, :], ALU.mult)\
                        .then_inc(s["mixing"], 1)
                    pool.wait_ge(s["mixing"], a.n)
                    pool.tensor_tensor(pair[:, k, 0, :], pair[:, k, 0, :], pair[:, k, 1, :], ALU.add)\
                        .then_inc(s["mixed"], 1)

                def mix_beside(it, k):
                    a = At(it, k, 3)
                    if pairwise and a.live:
                        mix(a)

                def refill(it, k, weighed):
                    pool.wait_ge(s["weighted"], weighed)
                    pool.sem_inc(s["passed"], 1)
                    if k % W == 0:
                        for j in range(W):
                            pool.wait_ge(arrived[k + j], it * 16)
                            pool.sem_inc(s["passed"], 1)
                        stage(it, k // W)
                    gather(k)
                    if k == 0:
                        encode(it - 1, 1)
                    if k == W:
                        encode(it, 0)

                stage(0, 0)
                stage(0, 1)
                encode(0, 0)
                for k in range(R):
                    gather(k)
                for k in range(3, R):
                    mix_beside(0, k)
                with pool.Fori(1, ET // R) as it:
                    for k in range(R):
                        a = At(it, k, R)
                        weigh(a)
                        if k >= 1:
                            refill(it, k - 1, a.t)
                        mix_beside(it, k)
                    refill(it, R - 1, it * R)
                for k in range(R):
                    weigh(At(ET // R, k, R))
                    if k == 0:
                        pool.wait_ge(s["weighted"], ET - R + 1)
                        encode(ET // R - 1, 1)
                    mix_beside(ET // R, k)

            @block.vector
            def _(dve):
                dve.memset(acc[:, :, :, :], 0.0).then_inc(s["cleared"], 1)
                dve.memset(mrun[:, :, :], -3e38).then_inc(s["cleared"], 1)
                dve.memset(lg[:, :, KC - 1], 1.0).then_inc(s["cleared"], 1)
                dve.wait_ge(s["cleared"], 3)
                dve.wait_ge(s["list_in"], 16)

                def code(a):
                    if a.slot % (R // 2):
                        return
                    half = slice(a.slot, a.slot + R // 2)
                    cols = slice(a.t, a.t + R // 2) if isinstance(a.t, int) else bass.ds(a.t, R // 2)
                    if not isinstance(a.t, int) or a.t >= R:
                        dve.wait_ge(s["coded"], a.round * 2 + (a.slot // (R // 2) - 1))
                    dve.tensor_tensor(bits[:, half, :], lst[:, cols, 0:1].to_broadcast([P, R // 2, CODE]),
                                      c["bits"][:, :, :].to_broadcast([P, R // 2, CODE]),
                                      ALU.bitwise_and).then_inc(s["bits_in"], 1)

                def differ(a):
                    k = a.slot % 2
                    mine = p_pair[:, k * F:(k + 1) * F]
                    dve.wait_ge(s["rowed"], a.n)
                    if not isinstance(a.t, int) or a.t >= 2:
                        dve.wait_ge(s["dotted"], a.t - 1)
                    dve.tensor_tensor(pair[:, k, 0, :], mine, got[:, a.slot, 0:F], ALU.subtract)
                    dve.tensor_tensor(pair[:, k, 1, :], mine, got[:, a.slot, GW:width], ALU.mult)\
                        .then_inc(s["differed"], 1)

                def dots(a):
                    dve.wait_ge(s["mixed"], a.n)
                    dve.tensor_reduce(dot[:, a.slot % 4, :],
                                      pair[:, a.slot % 2, 0, :].rearrange("p (h d) -> p h d", h=H),
                                      AX.X, ALU.add).then_inc(s["dotted"], 1)

                def join(a):
                    dve.wait_ge(s["termed"], a.n)
                    dve.tensor_tensor(whole[:, a.slot % 2, :], p_x[:, 0:H], got[:, a.slot, F:GW], ALU.add)\
                        .then_inc(s["joined"], 1)

                def leaky(a):
                    w = whole[:, a.slot % 2, :]
                    dve.wait_ge(s["joined"], a.n)
                    dve.scalar_tensor_tensor(out=lg[:, a.slot, 0:H], in0=w, scalar=SLOPE, in1=w,
                                             op0=ALU.mult, op1=ALU.max).then_inc(s["leaked"], 1)

                def offsets(a):
                    dve.wait_ge(s["offset"], a.n)
                    dve.tensor_tensor(below[:, a.slot % 2, :], p_z[:, 0:H], lg[:, a.slot, 0:H],
                                      ALU.subtract).then_inc(s["below_in"], 1)

                def maximum(a):
                    k = a.slot % 2
                    dve.wait_ge(s["spread"], a.n)
                    dve.tensor_reduce(tmax[:, k, :], p_max[:, :, :], AX.X, ALU.max)\
                        .then_inc(s["tmax_in"], 1)

                def rise(a):
                    k = a.slot % 2
                    dve.wait_ge(s["tmax_in"], a.n)
                    if not a.first:
                        dve.wait_ge(s["offset"], a.t)
                    run = node(mrun, a)
                    dve.tensor_tensor(drop[:, k, 0, :], tmax[:, k, :], run, ALU.subtract)\
                        .then_inc(s["rise_in"], 1)
                    dve.tensor_tensor(run, run, tmax[:, k, :], ALU.max).then_inc(s["mrun_in"], 1)

                def fade(a):
                    dve.wait_ge(s["scaled"], a.n)
                    if not a.first:
                        dve.wait_ge(s["added"], a.t)
                    dve.tensor_tensor(sums_of(a), sums_of(a),
                                      scale[:, a.slot % 4, :].unsqueeze(2).to_broadcast([P, H, VW]),
                                      ALU.mult).then_inc(s["faded"], 1)

                def add(a):
                    dve.wait_ge(s["sums"], a.n)
                    dve.wait_ge(s["faded"], a.n)
                    dve.tensor_tensor(sums_of(a), sums_of(a),
                                      p_sum[a.slot % len(p_sum)][:, 0:H * VW].rearrange("p (h d) -> p h d", h=H),
                                      ALU.add).then_inc(s["added"], 1)

                def sums_of(a):
                    return acc[:, bass.ds(a.tid, 1), :, :].rearrange("p a h d -> p (a h) d")

                plan = ((8, fade), (5, leaky), (7, offsets), (2, differ), (8, add), (6, maximum),
                        (3, dots), (4, join), (6, rise), (0, code)) if pairwise else \
                    ((3, leaky), (8, add), (0, code), (5, offsets), (4, maximum), (2, join),
                     (7, fade), (4, rise))
                steps(dve, run_stages(plan), mybir.EngineType.DVE)

            @block.scalar
            def _(act):
                act.wait_ge(s["list_in"], 16)

                def select(a):
                    k = a.slot % 2
                    if not isinstance(a.t, int) or a.t >= R:
                        act.wait_ge(s["sums"], a.t + (1 - R))
                    if not isinstance(a.t, int) or a.t >= 2:
                        act.wait_ge(s["selected"], a.t - 1)
                    act.sem_inc(s["held"], 1)
                    act.activation(apart[:, k, :], c["slot"][:, :], ACT.Abs, scale=-1.0,
                                   bias=col_of(lo, a.t)).then_inc(s["apart_in"], 1)
                    act.wait_ge(s["apart_in"], a.n)
                    act.activation(hot[:, a.slot, :], apart[:, k, :], ACT.Relu, scale=-1.0, bias=1.0)\
                        .then_inc(s["selected"], 1)

                def copy(a):
                    act.wait_ge(s["turned"], a.n)
                    act.activation(hot_t[:, a.slot, :], p_turn[:, 0:P], ACT.Copy)\
                        .then_inc(s["copied"], 1)

                def absolute(a):
                    d = pair[:, a.slot % 2, 0, :]
                    act.wait_ge(s["differed"], a.n)
                    act.activation(d, d, ACT.Abs).then_inc(s["absed"], 1)

                def turn_logits(a):
                    act.wait_ge(s["lgt"], a.n)
                    act.activation(lg_t[:, a.slot % 2, :], p_lgt[0:KC, 0:P], ACT.Copy)\
                        .then_inc(s["lgt_in"], 1)

                def ramp(a):
                    k = a.slot % 2
                    act.wait_ge(s["rise_in"], a.n)
                    act.activation(drop[:, k, 1, :], drop[:, k, 0, :], ACT.Relu).then_inc(s["ramped"], 1)
                    act.wait_ge(s["ramped"], a.n)
                    act.activation(scale[:, a.slot % 4, :], drop[:, k, 1, :], ACT.Exp, scale=-1.0)\
                        .then_inc(s["scaled"], 1)

                def weights(a):
                    act.wait_ge(s["below_in"], a.n)
                    act.activation(wv[:, a.slot % 4, :, DH:VW].rearrange("p h d -> p (h d)"),
                                   below[:, a.slot % 2, :], ACT.Exp, scale=-1.0).then_inc(s["ex_in"], 1)

                plan = ((7, weights), (2, absolute), (1, copy), (5, turn_logits), (0, select),
                        (6, ramp)) \
                    if pairwise else ((1, copy), (5, weights), (3, turn_logits), (0, select), (4, ramp))
                steps(act, run_stages(plan))

            @block.tensor
            def _(pe):
                def turn(a):
                    pe.wait_ge(s["selected"], a.n)
                    if not a.first:
                        pe.wait_ge(s["copied"], a.t)
                    pe.transpose(p_turn[:, 0:P], hot[:, a.slot, :], c["ident"][:, :])\
                        .then_inc(s["turned"], 1)

                def sums(a):
                    pe.wait_ge(s["weighted"], a.n)
                    if not isinstance(a.t, int) or a.t >= len(p_sum):
                        pe.wait_ge(s["added"], a.t + (1 - len(p_sum)))
                    pe.matmul(p_sum[a.slot % len(p_sum)][:, 0:H * VW], hot[:, a.slot, :],
                              wv[:, a.slot % 4, :, :].rearrange("p h d -> p (h d)"),
                              start=True, stop=True).then_inc(s["sums"], 1)

                def rows(a):
                    k = a.slot % 2
                    pe.wait_ge(arrived[a.slot], a.round * 16 + 16)
                    pe.wait_ge(s["copied"], a.n)
                    if not isinstance(a.t, int) or a.t >= 2:
                        pe.wait_ge(s["differed"], a.t - 1)
                    for i in range(3):
                        mm = pe.matmul(p_pair[:, k * F:(k + 1) * F], hot_t[:, a.slot, :],
                                       node(key_parts[i], a), start=(i == 0), stop=(i == 2))
                    mm.then_inc(s["rowed"], 1)

                def terms(a):
                    pe.wait_ge(arrived[a.slot], a.round * 16 + 16)
                    pe.wait_ge(s["copied"], a.n)
                    if not a.first:
                        pe.wait_ge(s["joined"], a.t)
                    for i in range(3):
                        mm = pe.matmul(p_x[:, 0:H], hot_t[:, a.slot, :], node(key8, a)[:, i * H:(i + 1) * H],
                                       start=(i == 0), stop=(not pairwise and i == 2))
                    if pairwise:
                        pe.wait_ge(s["dotted"], a.n)
                        mm = pe.matmul(p_x[:, 0:H], c["ident"][:, :], dot[:, a.slot % 4, :],
                                       start=False, stop=True)
                    mm.then_inc(s["termed"], 1)

                def turn_logits(a):
                    pe.wait_ge(s["leaked"], a.n)
                    pe.wait_ge(s["coded"], a.round * 2 + (1 + a.slot // (R // 2)))
                    if not a.first:
                        pe.wait_ge(s["lgt_in"], a.t)
                    pe.transpose(p_lgt[0:KC, 0:P], lg[:, a.slot, :], c["ident"][:, :])\
                        .then_inc(s["lgt"], 1)

                def offsets(a):
                    if not a.first:
                        pe.wait_ge(s["below_in"], a.t)
                    pe.wait_ge(s["mrun_in"], a.n)
                    pe.matmul(p_z[:, 0:H], hot_t[:, a.slot, :], node(mrun, a), start=True, stop=True)\
                        .then_inc(s["offset"], 1)

                def spread(a):
                    if not a.first:
                        pe.wait_ge(s["tmax_in"], a.t)
                    pe.wait_ge(s["lgt_in"], a.n)
                    for h in range(H):
                        mm = pe.matmul(p_max[:, h, :], c["sel"][:, h, :], lg_t[:, a.slot % 2, :],
                                       start=True, stop=True)
                    mm.then_inc(s["spread"], 1)

                plan = ((7, offsets), (6, spread), (1, turn), (5, turn_logits), (4, terms), (1, rows),
                        (7, sums)) if pairwise else \
                    ((4, spread), (5, offsets), (1, turn), (3, turn_logits), (2, terms), (6, sums))
                steps(pe, run_stages(plan), mybir.EngineType.PE)


def divide_and_add(nc, tag, x, acc, reload=None):
    with ExitStack() as st:
        m = Pack(nc, st)
        den = m.sb(f"den{tag}", [P, NT * H])
        ls = m.sem(f"divide_link{tag}")
        back = m.sem(f"back{tag}")
        rows = acc[:, :, :, :].rearrange("p t h d -> p (t h) d")
        with nc.Block() as block:
            @block.sync
            def _(sp):
                if reload is not None:
                    sp.dma_start(x[:, :, :], reload).then_inc(back, 16)

            @block.vector
            def _(dve):
                link = Link(dve, ls)
                link(dve.tensor_scalar(den[:, :], rows[:, :, DH], EPS_S, None, ALU.add))
                link(dve.reciprocal(den[:, :], den[:, :]))
                link(dve.tensor_tensor(rows[:, :, 0:DH], rows[:, :, 0:DH],
                                       den[:, :].unsqueeze(2).to_broadcast([P, NT * H, DH]), ALU.mult))
                if reload is not None:
                    dve.wait_ge(back, 16)
                flat = x[:, :, :].rearrange("p t (h d) -> p (t h) d", h=H)
                link(dve.tensor_tensor(flat, flat, rows[:, :, 0:DH], ALU.add))


def routed_ffn(nc, tag, c, x, mv, rstd, I, scatter):
    TG = 4
    with ExitStack() as st:
        m = Pack(nc, st)
        w1 = m.sb("w1", [P, FC, XP, HID])
        w2 = m.sb("w2", [P, HC, XP, F])
        wg = m.sb("wg", [P, FC, XP])
        bg = m.sb("bg", [1, XP])
        b1 = m.sb("b1", [P, XP, HC])
        b2 = m.sb("b2", [XP, F])
        xn = m.sb("xnf", [P, TG, F])
        xt = m.sb("xtf", [P, FC, TG * P])
        hs = m.sb("hidden", [P, 2, HC, TG * P])
        score = m.sb("score", [P, TG, XP])
        top8 = m.sb("top8", [P, TG, XP])
        topi = m.sb("topi", [P, TG, XP], U32)
        topf = m.sb("topf", [P, TG, XP])
        hit = m.sb("hit_x", [P, 2, TG, XP])
        mask = m.sb("mask_x", [P, TG, XP])
        mt = m.sb("mask_t", [XP, TG * P])
        tp = [m.ps(f"tp_x{i}", [P, 512]) for i in range(FC)]
        pg = m.ps("p_gate", [P, 512])
        pm = m.ps("p_mask", [P, 512])
        ph = [m.ps(f"p_hid{i}", [P, 512]) for i in range(2)]
        py = [m.ps(f"p_y{i}", [P, 512]) for i in range(2)]
        names = ("w_in", "xn_ready", "turned", "xt_ready", "gated", "gate_link", "masked",
                 "mask_turned", "mask_in", "hid", "gelued", "y", "taken", "hold")
        s = {n: m.sem(f"ffn_{n}{tag}") for n in names}
        GL = TG * 2 + 5

        def groups(eng, body):
            with eng.Fori(0, NT // TG) as g:
                body(g, TG)
            if NT % TG:
                body(NT // TG, NT % TG)

        with nc.Block() as block:
            @block.sync
            def _(sp):
                for f in range(FC):
                    sp.dma_start(w1[:, f, :, :], I["L0_ffn_W1"][:, f * P:(f + 1) * P, :]
                                 .rearrange("e p h -> p e h")).then_inc(s["w_in"], 16)
                for k in range(HC):
                    sp.dma_start(w2[:, k, :, :], I["L0_ffn_W2"][:, k * P:(k + 1) * P, :]
                                 .rearrange("e p d -> p e d")).then_inc(s["w_in"], 16)
                    sp.dma_start(b1[:, :, k], I["L0_ffn_b1"][:, k * P:(k + 1) * P]
                                 .rearrange("e p -> p e"), allow_slow_non_contiguous=True).then_inc(s["w_in"], 16)
                sp.dma_start(wg[:, :, :], I["L0_ffn_Wg"].rearrange("(f p) e -> p f e", p=P)).then_inc(s["w_in"], 16)
                sp.dma_start(bg[:, :], I["L0_ffn_bg"].rearrange("(a e) -> a e", a=1)).then_inc(s["w_in"], 16)
                sp.dma_start(b2[:, :], I["L0_ffn_b2"]).then_inc(s["w_in"], 16)

            @block.gpsimd
            def _(pool):
                scatter(pool)

            loaded = 16 * (FC + 2 * HC + 3)

            @block.vector
            def _(dve):
                def group(g, nt):
                    def tile(j):
                        return tile_of(x, g * TG + j)

                    for j in range(nt):
                        ins = dve.tensor_scalar(xn[:, j, :], tile(j), col_of(mv[:, :, 0], g * TG + j),
                                                col_of(rstd, g * TG + j), ALU.subtract, ALU.mult)
                    ins.then_inc(s["xn_ready"], 1)
                    n = [0]

                    def link(ins):
                        n[0] += 1
                        ins.then_inc(s["gate_link"], 1)
                        dve.wait_ge(s["gate_link"], g * GL + n[0])
                        dve.sem_inc(s["hold"], 1)

                    dve.wait_ge(s["gated"], g + 1)
                    link(dve.tensor_copy(score[:, 0:nt, :].rearrange("p t e -> p (t e)"), pg[:, 0:nt * XP]))
                    for j in range(nt):
                        link(dve.max(top8[:, j, :], score[:, j, :]))
                        link(dve.max_index(topi[:, j, :], top8[:, j, :], score[:, j, :]))
                    link(dve.tensor_copy(topf[:, 0:nt, :], topi[:, 0:nt, :]))
                    count = c["iota"][:, 0:XP].unsqueeze(1).to_broadcast([P, nt, XP])
                    for r in range(2):
                        link(dve.tensor_tensor(hit[:, r, 0:nt, :], count,
                                               topf[:, 0:nt, r:r + 1].to_broadcast([P, nt, XP]),
                                               ALU.is_equal))
                    link(dve.tensor_tensor(mask[:, 0:nt, :], hit[:, 0, 0:nt, :], hit[:, 1, 0:nt, :], ALU.add))
                    dve.sem_inc(s["masked"], 1)
                    for q in range((XP + 1) * nt):
                        e, j = q // nt - 1, q % nt
                        n_q = g * ((XP + 1) * TG) + q
                        dve.wait_ge(s["y"], n_q + 1)
                        if q >= nt:
                            dve.wait_ge(s["taken"], n_q - nt + 3)
                        if e < 0:
                            ins = dve.tensor_tensor(tile(j), tile(j), py[q % 2][:, 0:F], ALU.add)
                        else:
                            ins = dve.scalar_tensor_tensor(out=tile(j), in0=py[q % 2][:, 0:F],
                                                           scalar=mask[:, j, e:e + 1], in1=tile(j),
                                                           op0=ALU.mult, op1=ALU.add)
                        ins.then_inc(s["taken"], 1)
                dve.sem_inc(s["taken"], 2)
                groups(dve, group)

            @block.scalar
            def _(act):
                act.sem_inc(s["gelued"], 2)
                act.wait_ge(s["w_in"], loaded)

                def group(g, nt):
                    w = nt * P
                    for f in range(FC):
                        act.wait_ge(s["turned"], g * FC + f + 1)
                        act.activation(xt[:, f, 0:w], tp[f][:, 0:w], ACT.Copy).then_inc(s["xt_ready"], 1)
                    for e in range(XP):
                        for k in range(HC):
                            n = g * (XP * HC) + (e * HC + k)
                            act.wait_ge(s["hid"], n + 1)
                            act.activation(hs[:, e % 2, k, 0:w], ph[k % 2][:, 0:w], ACT.Gelu,
                                           bias=b1[:, e, k:k + 1]).then_inc(s["gelued"], 1)
                        if e == 0:
                            act.wait_ge(s["mask_turned"], g + 1)
                            act.activation(mt[:, 0:w], pm[0:XP, 0:w], ACT.Copy).then_inc(s["mask_in"], 1)
                groups(act, group)

            @block.tensor
            def _(pe):
                pe.wait_ge(s["w_in"], loaded)

                def group(g, nt):
                    w = nt * P

                    def up(e):
                        for k in range(HC):
                            pe.wait_ge(s["gelued"], g * (XP * HC) + (e * HC + k + 1))
                            for f in range(FC):
                                mm = pe.matmul(ph[k % 2][:, 0:w], w1[:, f, e, k * P:(k + 1) * P],
                                               xt[:, f, 0:w], start=(f == 0), stop=(f == FC - 1))
                            mm.then_inc(s["hid"], 1)

                    def down(e):
                        for j in range(nt):
                            q = (e + 1) * nt + j
                            if e < 0:
                                pe.wait_ge(s["mask_in"], g + 1)
                            elif j == 0:
                                pe.wait_ge(s["gelued"], g * (XP * HC) + ((e + 1) * HC + 2))
                            pe.wait_ge(s["taken"], g * ((XP + 1) * TG) + (q + 1))
                            cols = slice(j * P, (j + 1) * P)
                            if e < 0:
                                mm = pe.matmul(py[q % 2][:, 0:F], mt[:, cols], b2[:, :], start=True, stop=True)
                            else:
                                for k in range(HC):
                                    mm = pe.matmul(py[q % 2][:, 0:F], hs[:, e % 2, k, cols], w2[:, k, e, :],
                                                   start=(k == 0), stop=(k == HC - 1))
                            mm.then_inc(s["y"], 1)

                    pe.wait_ge(s["xn_ready"], g + 1)
                    for f in range(FC):
                        for j in range(nt):
                            mm = pe.transpose(tp[f][:, j * P:(j + 1) * P], xn[:, j, f * P:(f + 1) * P],
                                              c["ident"][:, :])
                        mm.then_inc(s["turned"], 1)
                    pe.wait_ge(s["xt_ready"], g * FC + FC)
                    for j in range(nt):
                        bank = pg[:, j * XP:(j + 1) * XP]
                        pe.matmul(bank, c["ones"][0:1, :], bg[:, :], start=True, stop=False)
                        for f in range(FC):
                            mm = pe.matmul(bank, xt[:, f, j * P:(j + 1) * P], wg[:, f, :],
                                           start=False, stop=(f == FC - 1))
                    mm.then_inc(s["gated"], 1)
                    up(0)
                    pe.wait_ge(s["masked"], g + 1)
                    for j in range(nt):
                        mm = pe.transpose(pm[0:XP, j * P:(j + 1) * P], mask[:, j, :], c["ident"][:, :])
                    mm.then_inc(s["mask_turned"], 1)
                    up(1)
                    down(-1)
                    down(0)
                    for e in range(1, XP):
                        if e + 1 < XP:
                            up(e + 1)
                        down(e)
                groups(pe, group)


def pair_weights(nc, m, c, W, a):
    wcat = m.sb("wcat1", [P, FC, 272])
    a45 = m.sb("a45", [P, 2, F])
    with ExitStack() as st:
        k = Pack(nc, st)
        av = k.sb("a_rows", [P, H, 5 * DH])
        vec = k.sb("a_sums", [P, 2, H, DH])
        tmp = k.sb("wtmp1", [P, H, DH])
        ld, ls = k.sem("w1_loaded"), k.sem("w1_link")
        with nc.Block() as block:
            @block.sync
            def _(sp):
                for f in range(FC):
                    sp.dma_start(wcat[:, f, 0:F].rearrange("p (h d) -> p h d", h=H),
                                 W[:, f * P:(f + 1) * P, :].rearrange("h p d -> p h d")).then_inc(ld, 16)
                sp.dma_start(av[:, :, :].rearrange("p h k -> p (h k)"),
                             a.rearrange("h k -> (h k)").partition_broadcast(P)).then_inc(ld, 16)

            @block.vector
            def _(dve):
                link = Link(dve, ls)
                part = lambda i: av[:, :, i * DH:(i + 1) * DH]
                heads = lambda r: r.rearrange("p (h d) -> p h d", h=H)
                dve.wait_ge(ld, 16 * (FC + 1))
                link(dve.tensor_tensor(vec[:, 0, :, :], part(1), part(2), ALU.add))
                link(dve.tensor_tensor(vec[:, 1, :, :], part(0), part(2), ALU.subtract))
                for i in range(2):
                    link(dve.tensor_copy(heads(a45[:, i, :]), part(3 + i)))
                    for f in range(FC):
                        link(dve.tensor_tensor(tmp[:, :, :], heads(wcat[:, f, 0:F]), vec[:, i, :, :], ALU.mult))
                        link(dve.tensor_reduce(wcat[:, f, F + i * H:F + (i + 1) * H], tmp[:, :, :],
                                               AX.X, ALU.add))
    return wcat, a45


def slice_weights(nc, m, c, I):
    w = {}
    w["log"] = m.sb("w_log", [P, FC, INNER])
    w["blog"] = m.sb("b_log", [1, INNER])
    w["fx"] = m.sb("w_fx", [P, FC, INNER])
    w["bfx"] = m.sb("b_fx", [1, INNER])
    w["qkv"] = m.sb("w_qkv", [SD, 3, SD])
    w["out"] = m.sb("w_out", [SD, H, F])
    w["bout"] = m.sb("b_out", [1, F])
    with ExitStack() as st:
        k = Pack(nc, st)
        wx = k.sb("w_x", [P, FC, INNER])
        wxt = k.sb("w_xt", [SD, H, F])
        bx = k.sb("b_x", [SD, H])
        ws = k.sb("w_slice", [SD, SG])
        bs = k.sb("b_slice", [1, SG])
        rt = k.sb("r_temp", [P, H])
        pt = [k.ps(f"p_wxt{i}", [P, 512]) for i in range(2)]
        pw = [k.ps(f"p_wlog{i}", [P, 512]) for i in range(FC)]
        pb = k.ps("p_blog", [P, 512])
        ld, ls, turned, copied, made = (k.sem(n) for n in ("w2_loaded", "w2_link", "wx_turned",
                                                          "wx_copied", "wlog_made"))
        with nc.Block() as block:
            @block.sync
            def _(sp):
                feat = lambda n: I[n].rearrange("(f p) n -> p f n", p=P)
                row = lambda n: I[n].rearrange("(a n) -> a n", a=1)
                sp.dma_start(wx[:, :, :], feat("L1_ffn_W_x")).then_inc(ld, 16)
                sp.dma_start(w["fx"][:, :, :], feat("L1_ffn_W_fx")).then_inc(ld, 16)
                sp.dma_start(w["bfx"][:, :], row("L1_ffn_b_fx")).then_inc(ld, 16)
                sp.dma_start(w["bout"][:, :], row("L1_ffn_b_out")).then_inc(ld, 16)
                sp.dma_start(bs[:, :], row("L1_ffn_b_slice")).then_inc(ld, 16)
                sp.dma_start(ws[:, :], I["L1_ffn_W_slice"]).then_inc(ld, 16)
                sp.dma_start(bx[:, :], I["L1_ffn_b_x"].rearrange("(h d) -> d h", d=SD),
                             allow_slow_non_contiguous=True).then_inc(ld, 16)
                for i, n in enumerate(("W_q", "W_k", "W_v")):
                    sp.dma_start(w["qkv"][:, i, :], I[f"L1_ffn_{n}"]).then_inc(ld, 16)
                sp.dma_start(w["out"][:, :, :], I["L1_ffn_W_out"].rearrange("(h d) n -> d h n", d=SD)).then_inc(ld, 16)
                sp.dma_start(rt[:, :], I["L1_ffn_temperature"].rearrange("a h b c -> (a h b c)")
                             .partition_broadcast(P)).then_inc(ld, 16)

            @block.tensor
            def _(pe):
                pe.wait_ge(ld, 16 * 12)
                for h in range(H):
                    if h >= 2:
                        pe.wait_ge(copied, h - 1)
                    for f in range(FC):
                        mm = pe.transpose(pt[h % 2][0:SD, f * P:(f + 1) * P],
                                          wx[:, f, h * SD:(h + 1) * SD], c["ident"][:, :])
                    mm.then_inc(turned, 1)
                pe.wait_ge(copied, H)
                for h in range(H):
                    cols = slice(h * SG, (h + 1) * SG)
                    for f in range(FC):
                        pe.matmul(pw[f][:, cols], wxt[:, h, f * P:(f + 1) * P], ws[:, :],
                                  start=True, stop=True)
                    pe.matmul(pb[0:1, cols], bx[:, h:h + 1], ws[:, :], start=True, stop=False)
                    mm = pe.matmul(pb[0:1, cols], c["ones"][0:1, 0:1], bs[:, :], start=False, stop=True)
                mm.then_inc(made, 1)

            @block.scalar
            def _(act):
                for h in range(H):
                    act.wait_ge(turned, h + 1)
                    act.activation(wxt[:, h, :], pt[h % 2][0:SD, 0:F], ACT.Copy).then_inc(copied, 1)

            @block.vector
            def _(dve):
                link = Link(dve, ls)
                dve.wait_ge(ld, 16 * 12)
                link(dve.tensor_scalar(rt[:, :], rt[:, :], 0.1, 5.0, ALU.max, ALU.min))
                link(dve.reciprocal(rt[:, :], rt[:, :]))
                dve.wait_ge(made, 1)
                heads = lambda r: r.rearrange("p (h g) -> p h g", h=H)
                for f in range(FC):
                    link(dve.tensor_tensor(heads(w["log"][:, f, :]), heads(pw[f][:, :]),
                                           rt[:, :].unsqueeze(2).to_broadcast([P, H, SG]), ALU.mult))
                link(dve.tensor_tensor(heads(w["blog"][:, :]), heads(pb[0:1, :]),
                                       rt[0:1, :].unsqueeze(2).to_broadcast([1, H, SG]), ALU.mult))
    return w


def slice_attention(nc, top, c, x, mv, rstd, w, out):
    with ExitStack() as st:
        m = Pack(nc, st)
        sw = m.sb("slice_w", [P, NT, INNER])
        mo = m.sb("mixed", [P, H // 2, F])
        with ExitStack() as st2:
            k = Pack(nc, st2)
            sx = k.sb("slice_xT", [P, FC, INNER])
            nrm = k.sb("slice_norm", [1, INNER])
            slice_sums(nc, c, x, mv, rstd, w, sw, sx, nrm)
            slice_mix(nc, c, w, sx, nrm, mo)
        slice_back(nc, c, x, w, sw, mo, out)


def slice_sums(nc, c, x, mv, rstd, w, sw, sx, nrm):
    U = 4
    with ExitStack() as st:
        m = Pack(nc, st)
        xn = m.sb("xns", [P, U, F])
        xt = m.sb("xts", [P, 2, FC, P])
        mx = m.sb("smax", [P, 2, H])
        ex = m.sb("sexp", [P, 2, INNER])
        sm = m.sb("ssum", [P, 2, H])
        rc = m.sb("srec", [P, 2, H])
        tp = [m.ps(f"tps_s{i}", [P, 512]) for i in range(2)]
        pl = [m.ps(f"p_logit{i}", [P, 512]) for i in range(2)]
        px = [m.ps(f"p_sx{i}", [P, 512]) for i in range(FC)]
        pn = m.ps("p_norm", [P, 512])
        names = ("xn_ready", "turned", "xt_ready", "logit", "max_in", "shifted", "exp_in", "sum_in",
                 "rec_in", "sw_in", "added",)
        s = {n: m.sem(f"ss_{n}") for n in names}
        heads = lambda r: r.rearrange("p (h g) -> p h g", h=H)
        wide = lambda r: r.unsqueeze(2).to_broadcast([P, H, SG])

        def run(eng, *plan):
            def body(it):
                for k in range(U):
                    for lag, stage in plan:
                        t = it * U + (k - lag)
                        if not isinstance(it, int) or 0 <= t < NT:
                            stage(t, (k - lag) % U)
            body(0)
            with eng.Fori(1, NT // U) as it:
                body(it)
            for it in range(NT // U, -(-(NT + 3) // U)):
                body(it)

        later = lambda t, n: not isinstance(t, int) or t >= n

        with nc.Block() as block:
            @block.vector
            def _(dve):
                def normal(t, k):
                    if later(t, U):
                        dve.wait_ge(s["added"], t - (U - 1))
                    dve.tensor_scalar(xn[:, k, :], tile_of(x, t), col_of(mv[:, :, 0], t),
                                      col_of(rstd, t), ALU.subtract, ALU.mult).then_inc(s["xn_ready"], 1)

                def shift(t, k):
                    k %= 2
                    dve.wait_ge(s["logit"], t + 1)
                    dve.tensor_reduce(mx[:, k, :], heads(pl[k][:, :]), AX.X, ALU.max).then_inc(s["max_in"], 1)
                    dve.wait_ge(s["max_in"], t + 1)
                    dve.tensor_tensor(heads(ex[:, k, :]), heads(pl[k][:, :]), wide(mx[:, k, :]),
                                      ALU.subtract).then_inc(s["shifted"], 1)

                def share(t, k):
                    k %= 2
                    dve.wait_ge(s["exp_in"], t + 1)
                    dve.tensor_reduce(sm[:, k, :], heads(ex[:, k, :]), AX.X, ALU.add).then_inc(s["sum_in"], 1)
                    dve.wait_ge(s["sum_in"], t + 1)
                    dve.reciprocal(rc[:, k, :], sm[:, k, :]).then_inc(s["rec_in"], 1)
                    dve.wait_ge(s["rec_in"], t + 1)
                    dve.tensor_tensor(heads(tile_of(sw, t)), heads(ex[:, k, :]), wide(rc[:, k, :]),
                                      ALU.mult).then_inc(s["sw_in"], 1)

                run(dve, (0, normal), (3, share), (2, shift))
                dve.wait_ge(s["added"], NT)
                for f in range(FC):
                    dve.tensor_copy(sx[:, f, :], px[f][:, :])
                dve.tensor_copy(nrm[:, :], pn[0:1, :])

            @block.scalar
            def _(act):
                def copy(t, k):
                    k %= 2
                    if later(t, 2):
                        act.wait_ge(s["logit"], t - 1)
                    act.wait_ge(s["turned"], t + 1)
                    act.activation(xt[:, k, :, :].rearrange("p f n -> p (f n)"), tp[k][:, 0:F],
                                   ACT.Copy).then_inc(s["xt_ready"], 1)

                def exponential(t, k):
                    k %= 2
                    act.wait_ge(s["shifted"], t + 1)
                    act.activation(ex[:, k, :], ex[:, k, :], ACT.Exp).then_inc(s["exp_in"], 1)

                run(act, (1, copy), (2, exponential))

            @block.tensor
            def _(pe):
                for bank, rows in ((px[0], P), (px[1], P), (pn, 1)):
                    pe.matmul(bank[0:rows, :], c["zeros"][:, 0:rows],
                              w["log"][:, 0, :], start=True, stop=False)

                def turn(t, k):
                    pe.wait_ge(s["xn_ready"], t + 1)
                    if later(t, 2):
                        pe.wait_ge(s["xt_ready"], t - 1)
                    for f in range(FC):
                        mm = pe.transpose(tp[k % 2][:, f * P:(f + 1) * P], xn[:, k, f * P:(f + 1) * P],
                                          c["ident"][:, :])
                    mm.then_inc(s["turned"], 1)

                def logits(t, k):
                    k %= 2
                    pe.wait_ge(s["xt_ready"], t + 1)
                    if later(t, 2):
                        pe.wait_ge(s["shifted"], t - 1)
                    pe.matmul(pl[k][:, :], c["ones"][0:1, :], w["blog"][:, :], start=True, stop=False)
                    for f in range(FC):
                        mm = pe.matmul(pl[k][:, :], xt[:, k, f, :], w["log"][:, f, :],
                                       start=False, stop=(f == FC - 1))
                    mm.then_inc(s["logit"], 1)

                def sums(t, k):
                    last = isinstance(t, int) and t == NT - 1
                    rows = TAIL if last else P
                    pe.wait_ge(s["sw_in"], t + 1)
                    mine = tile_of(sw, t)[0:rows, :]
                    for f in range(FC):
                        pe.matmul(px[f][:, :], xn[0:rows, k, f * P:(f + 1) * P], mine,
                                  start=False, stop=last)
                    pe.matmul(pn[0:1, :], c["ones"][0:rows, 0:1], mine,
                              start=False, stop=last).then_inc(s["added"], 1)

                run(pe, (1, turn), (3, sums), (1, logits))


def slice_mix(nc, c, w, sx, nrm, mo):
    with ExitStack() as st:
        m = Pack(nc, st)
        rn = m.sb("r_norm", [1, INNER])
        tok = m.sb("token_t", [SD, INNER])
        qt, kt = m.sb("q_t", [SD, INNER]), m.sb("k_t", [SD, INNER])
        vv = m.sb("v_rows", [SG, INNER])
        at = m.sb("att", [SG, INNER])
        a8 = m.sb("att8", [SG, 3, H])
        att_t, os_t = qt, kt
        mh = m.sb("mixed_h", [SG, H // 2, F])
        rb = at
        bank = [m.ps(f"pmix{i}", [P, 512]) for i in range(8)]
        dl, pl_, mv_ = m.sem("mix_dve"), m.sem("mix_pe"), m.sem("mix_moved")
        heads = lambda r: r.rearrange("p (h g) -> p h g", h=H)
        scale = float(SD) ** -0.5
        with nc.Block() as block:
            @block.vector
            def _(dve):
                link = Link(dve, dl)
                link(dve.tensor_scalar(rn[:, :], nrm[:, :], 1e-5, None, ALU.add))
                link(dve.reciprocal(rn[:, :], rn[:, :]))
                dve.wait_ge(pl_, 1)
                link(dve.tensor_copy(rb[:, :], bank[0][0:SD, :]))
                link(dve.tensor_tensor(tok[:, :], bank[1][0:SD, :], rb[:, :], ALU.mult))
                dve.wait_ge(pl_, 2)
                link(dve.tensor_copy(qt[:, :], bank[2][0:SD, :]))
                link(dve.tensor_copy(kt[:, :], bank[3][0:SD, :]))
                link(dve.tensor_copy(vv[:, :], bank[4][0:SG, :]))
                dve.wait_ge(pl_, 3)
                wide = lambda i: a8[:, i, :].unsqueeze(2).to_broadcast([SG, H, SG])
                link(dve.tensor_reduce(a8[:, 0, :], heads(bank[5][0:SG, :]), AX.X, ALU.max))
                link(dve.tensor_tensor(heads(at[:, :]), heads(bank[5][0:SG, :]), wide(0), ALU.subtract))
                dve.wait_ge(mv_, 1)
                link(dve.tensor_reduce(a8[:, 1, :], heads(at[:, :]), AX.X, ALU.add))
                link(dve.reciprocal(a8[:, 2, :], a8[:, 1, :]))
                link(dve.tensor_tensor(heads(at[:, :]), heads(at[:, :]), wide(2), ALU.mult))
                dve.wait_ge(pl_, 4)
                link(dve.tensor_copy(att_t[:, :], bank[6][0:SG, :]))
                dve.wait_ge(pl_, 5)
                link(dve.tensor_copy(os_t[:, :], bank[7][0:SD, :]))
                dve.wait_ge(pl_, 6)
                for i in range(4):
                    link(dve.tensor_copy(mh[:, i, :], bank[i][0:SG, F:2 * F]))
                for i in range(4):
                    link(dve.tensor_copy(mo[0:SG, i, :], bank[i][0:SG, 0:F]))
                dve.wait_ge(mv_, 17)

            @block.scalar
            def _(act):
                act.wait_ge(dl, 9)
                act.activation(at[:, :], at[:, :], ACT.Exp, scale=scale).then_inc(mv_, 1)

            @block.sync
            def _(sp):
                sp.wait_ge(dl, 18)
                sp.wait_ge(mv_, 1)
                sp.dma_start(mo[SG:P, :, :], mh[:, :, :]).then_inc(mv_, 16)
                sp.wait_ge(mv_, 17)

            @block.tensor
            def _(pe):
                pe.wait_ge(dl, 2)
                pe.matmul(bank[0][0:SD, :], c["ones"][0:1, 0:SD], rn[:, :], start=True, stop=True)
                for h in range(H):
                    hc = slice(h * SD, (h + 1) * SD)
                    for f in range(FC):
                        pe.matmul(bank[1][0:SD, hc], w["fx"][:, f, hc], sx[:, f, hc],
                                  start=(f == 0), stop=False)
                    mm = pe.matmul(bank[1][0:SD, hc], w["bfx"][:, hc], nrm[:, hc], start=False, stop=True)
                mm.then_inc(pl_, 1)
                pe.wait_ge(dl, 4)
                pe.matmul(bank[2][0:SD, :], w["qkv"][:, 0, :], tok[:, :], start=True, stop=True)
                pe.matmul(bank[3][0:SD, :], w["qkv"][:, 1, :], tok[:, :], start=True, stop=True)
                for h in range(H):
                    hc = slice(h * SD, (h + 1) * SD)
                    mm = pe.matmul(bank[4][0:SG, hc], tok[:, hc], w["qkv"][:, 2, :], start=True, stop=True)
                mm.then_inc(pl_, 1)
                pe.wait_ge(dl, 7)
                for h in range(H):
                    hc = slice(h * SD, (h + 1) * SD)
                    mm = pe.matmul(bank[5][0:SG, hc], qt[:, hc], kt[:, hc], start=True, stop=True)
                mm.then_inc(pl_, 1)
                pe.wait_ge(dl, 12)
                for h in range(H):
                    hc = slice(h * SD, (h + 1) * SD)
                    mm = pe.transpose(bank[6][0:SG, hc], at[:, hc], c["ident"][0:SG, 0:SG])
                mm.then_inc(pl_, 1)
                pe.wait_ge(dl, 13)
                for h in range(H):
                    hc = slice(h * SD, (h + 1) * SD)
                    mm = pe.matmul(bank[7][0:SD, hc], vv[:, hc], att_t[:, hc], start=True, stop=True)
                mm.then_inc(pl_, 1)
                pe.wait_ge(dl, 14)
                for h in range(H):
                    hc = slice(h * SD, (h + 1) * SD)
                    mm = pe.matmul(bank[h // 2][0:SG, (h % 2) * F:(h % 2 + 1) * F], os_t[:, hc],
                                   w["out"][:, h, :], start=True, stop=True)
                mm.then_inc(pl_, 1)


def slice_back(nc, c, x, w, sw, mo, out):
    C = INNER // P
    with ExitStack() as st:
        m = Pack(nc, st)
        wt = m.sb("sw_t", [P, 2, C, P])
        tp = [m.ps(f"tpb{i}", [P, 512]) for i in range(2)]
        po = [m.ps(f"p_out{i}", [P, 512]) for i in range(2)]
        here = m.sb("sw_here", [P, 2, INNER])
        names = ("here_in", "turned", "wt_in", "out_ready", "taken", "stored", "hold")
        s = {n: m.sem(f"sb_{n}") for n in names}
        with nc.Block() as block:
            @block.tensor
            def _(pe):
                def turn(t, k):
                    pe.wait_ge(s["wt_in"], t + 1)
                    pe.wait_ge(s["here_in"], t + 1)
                    for q in range(C):
                        mm = pe.transpose(tp[k][:, q * P:(q + 1) * P], here[:, k, q * P:(q + 1) * P],
                                          c["ident"][:, :])
                    mm.then_inc(s["turned"], 1)

                def multiply(t, k):
                    pe.wait_ge(s["wt_in"], t + 3)
                    pe.wait_ge(s["taken"], t + 1)
                    pe.matmul(po[k][:, 0:F], c["ones"][0:1, :], w["bout"][:, :], start=True, stop=False)
                    for q in range(C):
                        mm = pe.matmul(po[k][:, 0:F], wt[:, k, q, :], mo[:, q, :],
                                       start=False, stop=(q == C - 1))
                    mm.then_inc(s["out_ready"], 1)

                def body(t, k):
                    turn(t + 1, 1 - k)
                    multiply(t, k)
                turn(0, 0)
                pairs(pe, NT - 1, body)
                multiply(NT - 1, (NT - 1) % 2)

            @block.gpsimd
            def _(pool):
                pool.sem_inc(s["turned"], 2)

                def body(t, k):
                    pool.wait_ge(s["turned"], t + 1)
                    pool.sem_inc(s["hold"], 1)
                    pool.tensor_copy(here[:, k, :], tile_of(sw, t)).then_inc(s["here_in"], 1)
                pairs(pool, NT, body)

            @block.scalar
            def _(act):
                act.sem_inc(s["wt_in"], 2)

                def body(t, k):
                    act.wait_ge(s["turned"], t + 3)
                    if not isinstance(t, int) or t >= 2:
                        act.wait_ge(s["out_ready"], t - 1)
                    act.activation(wt[:, k, :, :].rearrange("p q n -> p (q n)"), tp[k][:, :],
                                   ACT.Copy).then_inc(s["wt_in"], 1)
                body(0, 0)
                body(1, 1)
                with act.Fori(1, NT // 2) as it:
                    body(it * 2, 0)
                    body(it * 2 + 1, 1)
                body(NT - 1, (NT - 1) % 2)

            @block.vector
            def _(dve):
                dve.sem_inc(s["taken"], 2)

                def body(t, k):
                    dve.wait_ge(s["out_ready"], t + 1)
                    dve.tensor_tensor(tile_of(x, t), tile_of(x, t), po[k][:, 0:F], ALU.add)\
                        .then_inc(s["taken"], 1)
                pairs(dve, NT, body)

            @block.sync
            def _(sp):
                step = (NT - 1) // 4
                for i in range(4):
                    sp.wait_ge(s["taken"], (i + 1) * step + 2)
                    sp.dma_start(node_dram(out[i * step * P:(i + 1) * step * P, :]),
                                 x[:, i * step:(i + 1) * step, :]).then_inc(s["stored"], 16)
                sp.wait_ge(s["taken"], NT + 2)
                sp.dma_start(out[(NT - 1) * P:N, :], x[0:TAIL, NT - 1, :]).then_inc(s["stored"], 16)
                sp.wait_ge(s["stored"], 80)


def node_dram(a):
    return a.rearrange("(t p) w -> p t w", p=P)


def attention_weights(nc, top, m, c, W, bW, a_src, a_dst, a_bias, x_in, x):
    wcat = m.sb("wcat0", [P, FC, 272])
    brow = m.sb("brow0", [1, 272])
    asrc, adst = m.sb("asrc", [P, F]), m.sb("adst", [P, F])
    tmp = m.sb("wtmp0", [P, F])
    ab = m.sb("abias", [1, H])
    ld, xl, cl, ls = m.sem("w0_loaded"), top.sem("x_loaded"), m.sem("x_cleared"), m.sem("w0_link")
    with nc.Block() as block:
        @block.sync
        def _(sp):
            for f in range(FC):
                sp.dma_start(wcat[:, f, 0:F].rearrange("p (h d) -> p h d", h=H),
                             W[:, f * P:(f + 1) * P, :].rearrange("h p d -> p h d")).then_inc(ld, 16)
            sp.dma_start(brow[:, 0:F], bW.rearrange("(a h) d -> a (h d)", a=1)).then_inc(ld, 16)
            sp.dma_start(asrc[:, :], a_src.rearrange("h d -> (h d)").partition_broadcast(P)).then_inc(ld, 16)
            sp.dma_start(adst[:, :], a_dst.rearrange("h d -> (h d)").partition_broadcast(P)).then_inc(ld, 16)
            sp.dma_start(ab[:, :], a_bias.rearrange("(a h) -> a h", a=1)).then_inc(ld, 16)
            sp.wait_ge(cl, 1)
            sp.dma_start(x[:, 0:NT - 1, :], node_dram(x_in[0:(NT - 1) * P, :])).then_inc(xl, 16)
            sp.dma_start(x[0:TAIL, NT - 1, :], x_in[(NT - 1) * P:N, :]).then_inc(xl, 16)
            sp.wait_ge(xl, 32)

        @block.vector
        def _(dve):
            link = Link(dve, ls)
            dve.memset(x[:, NT - 1, :], 0.0).then_inc(cl, 1)
            dve.wait_ge(ld, 96)
            for vec, at in ((asrc, F), (adst, F + H)):
                for f in range(FC):
                    link(dve.tensor_tensor(tmp[:, :], wcat[:, f, 0:F], vec[:, :], ALU.mult))
                    link(dve.tensor_reduce(wcat[:, f, at:at + H],
                                           tmp[:, :].rearrange("p (h d) -> p h d", h=H), AX.X, ALU.add))
                link(dve.tensor_tensor(tmp[0:1, :], brow[0:1, 0:F], vec[0:1, :], ALU.mult))
                link(dve.tensor_reduce(brow[0:1, at:at + H],
                                       tmp[0:1, :].rearrange("p (h d) -> p h d", h=H), AX.X, ALU.add))
            link(dve.tensor_tensor(brow[0:1, F + H:F + 2 * H], brow[0:1, F + H:F + 2 * H], ab[:, :],
                                   ALU.add))
    return wcat, brow


def store_table(nc, tag, c, table, rows, a5=None):
    G = 7
    width = GW if a5 is None else GW + F
    with ExitStack() as st:
        m = Pack(nc, st)
        s = m.sem(f"table_stored{tag}")
        made = m.sem(f"scaled_rows_made{tag}")
        stored = [m.sem(f"scaled_rows_stored{tag}{k}") for k in range(2)]
        ring = m.sb(f"scaled_rows{tag}", [P, 2, G, F]) if a5 is not None else None
        with nc.Block() as block:
            @block.sync
            def _(sp):
                sp.dma_start(node_dram(table[0:(NT - 1) * P, :])[:, :, 0:GW], rows[:, 0:NT - 1, :]).then_inc(s, 16)
                sp.dma_start(table[(NT - 1) * P:N, 0:GW], rows[0:TAIL, NT - 1, :]).then_inc(s, 16)
                pieces = range(0, width, P)
                for at in pieces:
                    w = min(P, width - at)
                    sp.dma_start(table[N:NT * P, at:at + w], c["zeros"][0:NT * P - N, 0:w]).then_inc(s, 16)
                if a5 is not None:
                    for g in range(NT // G):
                        k, t, n = g % 2, g * G, G if g < NT // G - 1 else G - 1
                        sp.wait_ge(made, g + 1)
                        sp.dma_start(node_dram(table[t * P:(t + n) * P, :])[:, :, GW:width],
                                     ring[:, k, 0:n, :]).then_inc(stored[k], 16)
                    sp.dma_start(table[(NT - 1) * P:N, GW:width], ring[0:TAIL, k, G - 1, :]).then_inc(s, 16)
                    for k in range(2):
                        sp.wait_ge(stored[k], 16 * -(-(NT // G - k) // 2))
                sp.wait_ge(s, 16 * (2 + len(pieces) + (a5 is not None)))

            @block.vector
            def _(dve):
                for g in range(NT // G if a5 is not None else 0):
                    if g >= 2:
                        dve.wait_ge(stored[g % 2], 16 * (g // 2))
                    dve.tensor_tensor(ring[:, g % 2, :, :], rows[:, g * G:(g + 1) * G, 0:F],
                                      a5.unsqueeze(1).to_broadcast([P, G, F]), ALU.mult).then_inc(made, 1)


def split3(nc, tag, key8, near8, rest):
    with ExitStack() as st:
        sem = Pack(nc, st).sem(f"split_link{tag}")
        with nc.Block() as block:
            @block.vector
            def _(dve):
                link = Link(dve, sem)
                part = lambda i: key8[:, :, i * H:(i + 1) * H]
                link(dve.tensor_copy(part(0), near8[:, :, :]))
                link(dve.tensor_tensor(rest[:, :, :], near8[:, :, :], part(0), ALU.subtract))
                link(dve.tensor_copy(part(1), rest[:, :, :]))
                link(dve.tensor_tensor(rest[:, :, :], rest[:, :, :], part(1), ALU.subtract))
                link(dve.tensor_copy(part(2), rest[:, :, :]))


def split_rows(eng, first, count, rows, parts, rest, link, hold, ready):
    K = 5

    def body(i, k):
        t = i + first

        def after(ins, n):
            ins.then_inc(link, 1)
            eng.wait_ge(link, i * K + n)
            eng.sem_inc(hold, 1)
        eng.wait_ge(ready, t + 1)
        eng.sem_inc(hold, 1)
        h = tile_of(rows, t)[:, 0:F]
        after(eng.tensor_copy(tile_of(parts[0], t), h), 1)
        after(eng.tensor_tensor(rest[:, k, :], h, tile_of(parts[0], t), ALU.subtract), 2)
        after(eng.tensor_copy(tile_of(parts[1], t), rest[:, k, :]), 3)
        after(eng.tensor_tensor(rest[:, k, :], rest[:, k, :], tile_of(parts[1], t), ALU.subtract), 4)
        after(eng.tensor_copy(tile_of(parts[2], t), rest[:, k, :]), 5)
    pairs(eng, count, body)


def build(nc, I, out):
    with ExitStack() as whole:
        Pack.whole = whole
        Pack.layer = ([], whole.enter_context(ExitStack()))
        top = Pack(nc, whole)
        c = constants(nc, top)
        x = top.sb("x", [P, NT, F])
        mv = top.sb("mv", [P, NT, 2])
        rstd = top.sb("rstd", [P, NT])
        tid = [top.sb(f"tid{i}", [1, ET], I32) for i in range(2)]
        table = nc.dram_tensor("table", (NT * P, GW), F32).ap()
        with ExitStack() as sort_stack:
            so = Pack(nc, sort_stack)
            triangles(nc, so, c)
            orders = [Order(nc, so, "A", I["dst"], I["src"]), Order(nc, so, "B", I["src"], I["dst"])]
            stage = [(so.sb(f"sidx{i}", [LANES, 2, RING], I32), so.sb(f"spay{i}", [LANES, 2, RING, 2], I32))
                     for i in range(2)]
            with ExitStack() as st:
                m = Pack(nc, st)
                wcat, brow = attention_weights(nc, top, m, c, I["L0_gnn_W"], I["L0_gnn_bW"],
                                               I["L0_gnn_a_src"], I["L0_gnn_a_dst"],
                                               I["L0_gnn_a_bias"], I["x"], x)
                sort_positions(nc, "A", c, orders[0], tid[0])
                norm_stats(nc, top, "0", x, mv, rstd)
                rows = m.sb("rows0", [P, NT, GW])
                near8 = m.sb("near8", [P, NT, H])
                key8 = m.sb("key8", [P, NT, 3 * H], BF16)
                with ExitStack() as st2:
                    b2 = sort_buffers(nc, st2, "B", orders[1])

                    def evac(act, t, k, ps):
                        act.activation(tile_of(rows, t), ps[:, 0:GW], ACT.Copy)
                        return act.activation(tile_of(near8, t), ps[:, GW:GW + H], ACT.Copy)
                    project(nc, "0", c, x, mv, rstd, wcat, brow, 272, evac, extra={
                        "vector": lambda dve, _: order_vector(dve, orders[1], b2, c, tid[1]),
                        "tensor": lambda pe: order_tensor(pe, orders[1], b2, c),
                        "gpsimd": lambda pool, _: order_scatter(pool, orders[0], stage[0]),
                    })
                store_table(nc, "0", c, table, rows)
                split3(nc, "0", key8, near8, m.sb("rest8", [P, NT, H]))
                acc = rows[:, :, :].rearrange("p t (h d) -> p t h d", h=H)
                edge_phase(nc, "0", c, orders[0], tid[0], table, acc, key8)
                divide_and_add(nc, "0", x, acc)
            norm_stats(nc, top, "1", x, mv, rstd)
            routed_ffn(nc, "1", c, x, mv, rstd, I, lambda pool: order_scatter(pool, orders[1], stage[1]))
        end_layer(nc)
        saved = nc.dram_tensor("saved_x", (NT * P, F), F32).ap()
        with ExitStack() as st:
            m = Pack(nc, st)
            norm_stats(nc, top, "2", x, mv, rstd, save=saved)
            wcat, a45 = pair_weights(nc, m, c, I["L1_gnn_W"], I["L1_gnn_a"])
            rows = m.sb("rows1", [P, NT, GW])
            near8 = m.sb("near8_1", [P, NT, H])
            key8 = m.sb("key8_1", [P, NT, 3 * H], BF16)
            place = x[:, :, :].bitcast(BF16)
            parts = [place[:, :, 0:F], place[:, :, F:2 * F], m.sb("part3", [P, NT, F], BF16)]
            mine = 20
            rest = [m.sb(f"rest_rows{i}", [P, 2, F]) for i in range(2)]
            link, hold = ([m.sem(f"split_rows_{n}{i}") for i in range(2)] for n in ("link", "hold"))

            def evac(act, t, k, ps):
                act.activation(tile_of(rows, t), ps[:, 0:GW], ACT.Copy)
                return act.activation(tile_of(near8, t), ps[:, GW:GW + H], ACT.Copy)
            project(nc, "2", c, x, mv, rstd, wcat, None, 272, evac, extra={
                "vector": lambda dve, ready: split_rows(dve, mine, NT - mine, rows, parts, rest[1],
                                                        link[1], hold[1], ready),
                "tensor": lambda pe: None,
                "gpsimd": lambda pool, ready: split_rows(pool, 0, mine, rows, parts, rest[0],
                                                         link[0], hold[0], ready),
            })
            pair_table = nc.dram_tensor("pair_table", (NT * P, GW + F), F32).ap()
            store_table(nc, "2", c, pair_table, rows, a45[:, 1, :])
            split3(nc, "2", key8, near8, m.sb("rest8_1", [P, NT, H]))
            acc = rows[:, :, :].rearrange("p t (h d) -> p t h d", h=H)
            edge_phase(nc, "2", c, orders[1], tid[1], pair_table, acc, key8, parts, a45)
            divide_and_add(nc, "2", x, acc, reload=node_dram(saved))
        with ExitStack() as st:
            m = Pack(nc, st)
            norm_stats(nc, top, "3", x, mv, rstd)
            w = slice_weights(nc, m, c, I)
            slice_attention(nc, top, c, x, mv, rstd, w, out)


_INS = ['x', 'src', 'dst', 'L0_gnn_W', 'L0_gnn_bW', 'L0_gnn_a_src', 'L0_gnn_a_dst', 'L0_gnn_a_bias',
        'L0_ffn_Wg', 'L0_ffn_bg', 'L0_ffn_W1', 'L0_ffn_b1', 'L0_ffn_W2', 'L0_ffn_b2', 'L1_gnn_W',
        'L1_gnn_a', 'L1_ffn_W_fx', 'L1_ffn_b_fx', 'L1_ffn_W_x', 'L1_ffn_b_x', 'L1_ffn_W_slice',
        'L1_ffn_b_slice', 'L1_ffn_W_q', 'L1_ffn_W_k', 'L1_ffn_W_v', 'L1_ffn_W_out', 'L1_ffn_b_out',
        'L1_ffn_temperature']


def kernel(**inputs):
    import numpy as _np
    import concourse.bacc as _bacc
    from concourse import mybir as _mybir
    from concourse.bass_utils import run_bass_kernel_spmd as _run

    nc = _bacc.Bacc("TRN2", target_bir_lowering=False, num_devices=1)
    arrays, args = {}, {}
    for name in _INS:
        a = _np.ascontiguousarray(inputs[name])
        arrays[f"in_{name}_dram"] = a
        args[name] = nc.dram_tensor(f"in_{name}_dram", a.shape, _mybir.dt.from_np(a.dtype),
                                    kind="ExternalInput").ap()
    out = nc.dram_tensor("out_0_dram", (N, F), _mybir.dt.float32, kind="ExternalOutput").ap()
    build(nc, args, out)
    r = _run(nc, [arrays], core_ids=[0])
    return r.results[0]["out_0_dram"]
```
